# Optimizing a Trainium2 kernel written in Bass

```python
import numpy as np
import jax
import jax.numpy as jnp

def _softmax(x, axis=-1):
    return jax.nn.softmax(x, axis=axis)

def _gelu(x):
    return jax.nn.gelu(x, approximate=True)

def _silu(x):
    return jax.nn.silu(x)

def _sigmoid(x):
    return jax.nn.sigmoid(x)

def _layernorm(x, axis=-1, eps=1e-05):
    m = jnp.mean(x, axis=axis, keepdims=True)
    v = jnp.var(x, axis=axis, keepdims=True)
    return (x - m) / jnp.sqrt(v + eps)

def _scatter_add(tgt, idx, src, axis=0):
    return tgt.at[idx].add(src)

def _segment_sum(src, seg, n):
    return jax.ops.segment_sum(src, seg, n)
kernel_name = 'mk_xattn_seq_d1_seqx_r4_0fcf36'

def setup_inputs(seed: int=0):
    np.random.seed(seed)
    _w = jnp.asarray

    def _rec_inputs():
        import jax
        import jax.numpy as jnp
        _rk = jax.random.key(seed)
        x = -0.0002928 + 1 * jax.random.normal(jax.random.fold_in(_rk, 1), (16, 256, 512), jnp.float32)
        _lenS = 256 - jax.random.randint(jax.random.fold_in(_rk, 7), (16,), 0, max(1, 256 // 4) + 1, jnp.int32)
        _lenS2 = 256 - jax.random.randint(jax.random.fold_in(_rk, 8), (16,), 0, max(1, 256 // 4) + 1, jnp.int32)
        _ctx_2048P = jax.random.normal(jax.random.fold_in(_rk, 11), (16, 16, 512), jnp.float32)
        _ctx_2048c = jax.random.dirichlet(jax.random.fold_in(_rk, 511), 0.3 * jnp.ones((16,), jnp.float32), (16, 256))
        _ctx_2048t = jnp.einsum('bsk,bkd->bsd', _ctx_2048c, _ctx_2048P)
        _ctx_2048t = _ctx_2048t * jax.lax.rsqrt(jnp.mean(jnp.square(_ctx_2048t)) + 1e-12) * 0.953939
        ctx_2048 = -1.39393e-06 + 0.999914 * (_ctx_2048t + 0.3 * jax.random.normal(jax.random.fold_in(_rk, 611), (16, 256, 512), jnp.float32))
        return (x, ctx_2048)
    x, ctx_2048 = _rec_inputs()

    def _L0_xattn_setup():
        import math
        import jax, jax.numpy as jnp
        import numpy as np
        C = 256
        H = 16
        DH = C // H
        EPS = 1e-05

        def pos_enc(c, T, dtype):
            pos = jnp.arange(T, dtype=jnp.float32)[:, None]
            div = jnp.exp(jnp.arange(0, c, 2, dtype=jnp.float32) * (-math.log(10000.0) / c))
            ang = pos * div
            pe = jnp.zeros((T, c), dtype=jnp.float32)
            pe = pe.at[:, 0::2].set(jnp.sin(ang)).at[:, 1::2].set(jnp.cos(ang))
            return pe.T.astype(dtype)

        def layer_norm(x, g, b):
            mu = jnp.mean(x, axis=-1, keepdims=True)
            var = jnp.mean(jnp.square(x - mu), axis=-1, keepdims=True)
            return (x - mu) * jax.lax.rsqrt(var + EPS) * g + b
        key = jax.random.key(seed)
        ks = jax.random.split(key, 16)
        s = 1.0 / math.sqrt(C)
        inp = {'zt_prev': jax.random.normal(ks[0], (2, C, 512), jnp.float32), 'za': jax.random.normal(ks[1], (2, C, 512), jnp.float32), 'Wq': jax.random.normal(ks[2], (C, C), jnp.float32) * s, 'Wk': jax.random.normal(ks[3], (C, C), jnp.float32) * s, 'Wv': jax.random.normal(ks[4], (C, C), jnp.float32) * s, 'Wo': jax.random.normal(ks[5], (C, C), jnp.float32) * s, 'ln_q_g': jnp.ones((C,), jnp.float32), 'ln_q_b': jnp.zeros((C,), jnp.float32), 'ln_kv_g': jnp.ones((C,), jnp.float32), 'ln_kv_b': jnp.zeros((C,), jnp.float32), 'ffn_ln_g': jnp.ones((C,), jnp.float32), 'ffn_ln_b': jnp.zeros((C,), jnp.float32), 'W1': jax.random.normal(ks[6], (C, 2 * C), jnp.float32) * s, 'b1': jnp.zeros((2 * C,), jnp.float32), 'W2': jax.random.normal(ks[7], (2 * C, C), jnp.float32) * (1.0 / math.sqrt(2 * C)), 'b2': jnp.zeros((C,), jnp.float32)}
        return inp
    _L0_xattn_all = _L0_xattn_setup()
    _L0_xattn_in = {k: v for k, v in _L0_xattn_all.items() if k in ('Wq', 'Wk', 'Wv', 'Wo', 'ln_q_g', 'ln_q_b', 'ln_kv_g', 'ln_kv_b', 'ffn_ln_g', 'ffn_ln_b', 'W1', 'b1', 'W2', 'b2')}
    del _L0_xattn_all
    return {'x': x, 'ctx_2048': ctx_2048, 'L0_xattn_Wq': _L0_xattn_in['Wq'], 'L0_xattn_Wk': _L0_xattn_in['Wk'], 'L0_xattn_Wv': _L0_xattn_in['Wv'], 'L0_xattn_Wo': _L0_xattn_in['Wo'], 'L0_xattn_ln_q_g': _L0_xattn_in['ln_q_g'], 'L0_xattn_ln_q_b': _L0_xattn_in['ln_q_b'], 'L0_xattn_ln_kv_g': _L0_xattn_in['ln_kv_g'], 'L0_xattn_ln_kv_b': _L0_xattn_in['ln_kv_b'], 'L0_xattn_ffn_ln_g': _L0_xattn_in['ffn_ln_g'], 'L0_xattn_ffn_ln_b': _L0_xattn_in['ffn_ln_b'], 'L0_xattn_W1': _L0_xattn_in['W1'], 'L0_xattn_b1': _L0_xattn_in['b1'], 'L0_xattn_W2': _L0_xattn_in['W2'], 'L0_xattn_b2': _L0_xattn_in['b2']}

def reference(x, ctx_2048, L0_xattn_Wq, L0_xattn_Wk, L0_xattn_Wv, L0_xattn_Wo, L0_xattn_ln_q_g, L0_xattn_ln_q_b, L0_xattn_ln_kv_g, L0_xattn_ln_kv_b, L0_xattn_ffn_ln_g, L0_xattn_ffn_ln_b, L0_xattn_W1, L0_xattn_b1, L0_xattn_W2, L0_xattn_b2):
    import jax
    import jax.numpy as jnp

    def _L0_xattn_ref(zt_prev, za, Wq, Wk, Wv, Wo, ln_q_g, ln_q_b, ln_kv_g, ln_kv_b, ffn_ln_g, ffn_ln_b, W1, b1, W2, b2):
        import math
        import jax, jax.numpy as jnp
        import numpy as np
        C = 256
        H = 16
        DH = C // H
        EPS = 1e-05

        def pos_enc(c, T, dtype):
            pos = jnp.arange(T, dtype=jnp.float32)[:, None]
            div = jnp.exp(jnp.arange(0, c, 2, dtype=jnp.float32) * (-math.log(10000.0) / c))
            ang = pos * div
            pe = jnp.zeros((T, c), dtype=jnp.float32)
            pe = pe.at[:, 0::2].set(jnp.sin(ang)).at[:, 1::2].set(jnp.cos(ang))
            return pe.T.astype(dtype)

        def layer_norm(x, g, b):
            mu = jnp.mean(x, axis=-1, keepdims=True)
            var = jnp.mean(jnp.square(x - mu), axis=-1, keepdims=True)
            return (x - mu) * jax.lax.rsqrt(var + EPS) * g + b
        B, _, Tq = zt_prev.shape
        Tk = za.shape[-1]
        q = jnp.transpose(zt_prev + pos_enc(C, Tq, zt_prev.dtype)[None], (0, 2, 1))
        kv = jnp.transpose(za + pos_enc(C, Tk, za.dtype)[None], (0, 2, 1))
        q = layer_norm(q, ln_q_g, ln_q_b)
        kv = layer_norm(kv, ln_kv_g, ln_kv_b)

        def split(x):
            Bt, T, _ = x.shape
            return jnp.transpose(x.reshape(Bt, T, H, DH), (0, 2, 1, 3))
        Q = split(q @ Wq)
        K = split(kv @ Wk)
        V = split(kv @ Wv)
        attn = jnp.einsum('bhqd,bhkd->bhqk', Q, K) / math.sqrt(DH)
        ctx = jnp.einsum('bhqk,bhkd->bhqd', jax.nn.softmax(attn, axis=-1), V)
        ctx = jnp.transpose(ctx, (0, 2, 1, 3)).reshape(B, Tq, C)
        y = ctx @ Wo
        r = y + q
        h = layer_norm(r, ffn_ln_g, ffn_ln_b)
        h = jax.nn.gelu(h @ W1 + b1, approximate=False) @ W2 + b2
        out = h + r
        return jnp.transpose(out, (0, 2, 1))
    x = _L0_xattn_ref(x, ctx_2048, L0_xattn_Wq, L0_xattn_Wk, L0_xattn_Wv, L0_xattn_Wo, L0_xattn_ln_q_g, L0_xattn_ln_q_b, L0_xattn_ln_kv_g, L0_xattn_ln_kv_b, L0_xattn_ffn_ln_g, L0_xattn_ffn_ln_b, L0_xattn_W1, L0_xattn_b1, L0_xattn_W2, L0_xattn_b2)
    return x

_drawn_inputs = setup_inputs


def setup_inputs(seed=0):
    import zlib

    import numpy as np

    out = dict(_drawn_inputs(seed))
    spreads = {'L0_xattn_ln_q_g': (1.0, 0.2),
     'L0_xattn_ln_q_b': (0.0, 0.1),
     'L0_xattn_ln_kv_g': (1.0, 0.2),
     'L0_xattn_ln_kv_b': (0.0, 0.1),
     'L0_xattn_ffn_ln_g': (1.0, 0.2),
     'L0_xattn_ffn_ln_b': (0.0, 0.1),
     'L0_xattn_b1': (0.0, 0.1),
     'L0_xattn_b2': (0.0, 0.1)}
    factors = {}
    for name, (base, spread) in spreads.items():
        noise = np.random.default_rng([zlib.crc32(name.encode()), seed]).standard_normal(out[name].shape)
        drawn = base * np.exp(spread * noise) if base else spread * noise
        out[name] = jnp.asarray(drawn.astype(out[name].dtype))
    for name, factor in factors.items():
        out[name] = (out[name] * factor).astype(out[name].dtype)
    return out
```

```python
from contextlib import ExitStack

import concourse.bass as bass
from concourse import mybir

F32 = mybir.dt.float32
F32R = mybir.dt.float32r
ALU = mybir.AluOpType
ACT = mybir.ActivationFunctionType
AX_X = mybir.AxisListType.X

P = 128
D = 16
HG = 4
EPS = 1e-5
TERMS = 4
ZROW = TERMS * D
MROW = ZROW + 1
DMA = 16


def xattn_kernel(nc, x, ctx_in, Wq, Wk, Wv, Wo, ln_q_g, ln_q_b, ln_kv_g, ln_kv_b,
                 ffn_g, ffn_b, W1, b1, W2, b2, pos, out):
    B, C, T = x.shape
    H = C // D
    CT = C // P
    KC = T // P
    NG = H // HG
    STEPS = NG * KC
    UNITS = STEPS * HG
    F = W1.shape[1]
    FT = F // P
    GPT = NG // CT
    LEAD = KC + 1
    STACK = 2 * TERMS * HG * DMA
    PLACED = 2 * HG * DMA
    SCALE = float(D) ** -0.5

    r_dram = nc.dram_tensor("r_scratch", [B, C, T], F32, kind="Internal").ap()

    with ExitStack() as es:
        def sb(name, shape, dt=F32):
            return es.enter_context(nc.sbuf_tensor(name, shape, dt))

        def bank(name, shape=(P, 512)):
            return es.enter_context(nc.psum_tensor(name, list(shape), F32))

        def sem(name):
            return es.enter_context(nc.semaphore(name))

        ident = sb("ident", [P, P])
        neg_half = sb("neg_half", [P, KC])
        pe_tab = sb("pe_tab", [P, CT, T])
        w_q, w_k, w_v, w_o = (sb(n, [P, CT, C]) for n in ("w_q", "w_k", "w_v", "w_o"))
        w_1 = sb("w_1", [P, CT, F])
        w_2 = sb("w_2", [P, FT, C])
        vecs = sb("vecs", [P, 10 * CT])
        b1_col = sb("b1_col", [P, FT])
        gq, bq, gk, bk, gf, bf, b2_col = (vecs[:, CT * i:CT * i + CT] for i in range(7))

        x_in = sb("x_in", [P, CT, T])
        kv_in = sb("kv_in", [P, CT, T])
        tok = {"k": sb("tok_k", [P, KC, C]), "q": sb("tok_q", [P, KC, C])}
        stat = {"k": sb("stat_k", [P, KC, 6]), "q": sb("stat_q", [P, KC, 6])}
        mv = {"k": sb("mv_k", [P, KC, 2]), "q": sb("mv_q", [P, KC, 2])}
        rstd = {"k": sb("rstd_k", [P, KC]), "q": sb("rstd_q", [P, KC])}
        ln = {"k": sb("ln_k", [P, CT, T]), "q": sb("ln_q", [P, CT, T])}
        hi = {"k": sb("hi_k", [P, CT, T], F32R), "q": sb("hi_q", [P, CT, T], F32R)}
        lo = {"k": sb("lo_k", [P, CT, T], F32R), "q": sb("lo_q", [P, CT, T], F32R)}
        stack = {"k": sb("stack_k", [P, H, T], F32R), "q": sb("stack_q", [P, H, T], F32R)}
        v_ones = sb("v_ones", [P, KC, H, 2 * D])
        probs = sb("probs", [P, 2, HG, T])
        neg_max = sb("neg_max", [P, 2, HG * KC])
        m_hi = sb("m_hi", [HG * KC, P], F32R)
        m_lo = sb("m_lo", [HG * KC, P], F32R)
        pv_sb = sb("pv_sb", [P, 2, T])
        ctx_raw = sb("ctx_raw", [P, CT, T])
        row_sum = sb("row_sum", [P, CT, T])
        q_res = sb("q_res", [P, CT, T])
        r_out = sb("r_out", [P, CT, T])

        sc_ps = [bank("sc_ps0"), bank("sc_ps1")]
        mx_ps = [bank("mx_ps0"), bank("mx_ps1")]
        pv_ps = bank("pv_ps")
        tr_ps = bank("tr_ps")
        pj_ps = bank("pj_ps")
        xc_ps = bank("xc_ps")

        consts = sem("consts")
        weights = sem("weights")
        loaded = {"k": sem("kv_loaded"), "q": sem("x_loaded")}
        pos_added = {"k": sem("kv_pos_added"), "q": sem("x_pos_added")}
        tr_in = {"k": sem("k_tr_in"), "q": sem("q_tr_in")}
        tok_ready = {"k": sem("k_tok"), "q": sem("q_tok")}
        bn_done = {"k": sem("k_bn"), "q": sem("q_bn")}
        stat_done = {"k": sem("k_stat"), "q": sem("q_stat")}
        rstd_step = {"k": sem("k_rstd"), "q": sem("q_rstd")}
        normed = {"k": sem("k_normed"), "q": sem("q_normed")}
        tr_out = {"k": sem("k_tr_out"), "q": sem("q_tr_out")}
        ln_done = {"k": sem("k_ln"), "q": sem("q_ln")}
        proj = {"k": sem("k_proj"), "q": sem("q_proj")}
        hi_done = {"k": sem("k_hi"), "q": sem("q_hi")}
        lo_done = {"k": sem("k_lo"), "q": sem("q_lo")}
        stacked = [sem(f"stacked{g}") for g in range(NG)]
        v_made = sem("v_made")
        v_done = sem("v_done")
        mx_made = sem("mx_made")
        mx_done = sem("mx_done")
        mt_made = sem("mt_made")
        mhi_done = sem("mhi_done")
        mlo_done = sem("mlo_done")
        m_placed = [sem(f"m_placed{g}") for g in range(NG)]
        sc_made = sem("sc_made")
        exp_done = sem("exp_done")
        pv_made = sem("pv_made")
        pv_out = sem("pv_out")
        ctx_placed = [sem(f"ctx_placed{g}") for g in range(NG)]
        inverted = sem("inverted")
        ctx_done = sem("ctx_done")
        wo_made = sem("wo_made")
        q_kept = sem("q_kept")
        r_done = sem("r_done")
        r_stored = sem("r_stored")

        def wait_apart(eng, semaphore, value):
            if not isinstance(value, int):
                value = eng.to_reg(value)
            eng.wait_ge(consts, 1)
            eng.wait_ge(semaphore, value)

        def unit_of(b, s, j):
            return b * UNITS + s * HG + j

        src = {"k": kv_in, "q": x_in}
        gain, bias = {"k": gk, "q": gq}, {"k": bk, "q": bq}
        w_of = {"k": w_k, "q": w_q}

        with nc.Block() as block:
            @block.sync
            def _(sp):
                def load(b, n):
                    if not (isinstance(b, int) and b == 0):
                        wait_apart(sp, tr_in[n], b * 2)
                    d = {"k": ctx_in, "q": x}[n]
                    sp.dma_start(src[n][:, :, :], d[b].rearrange("(t p) n -> p t n", p=P)
                                 ).then_inc(loaded[n], DMA)

                def fill_stack(b, g):
                    t, half = g // GPT, g % GPT
                    wait_apart(sp, lo_done["k"], b * 2 + t + 1)
                    wait_apart(sp, lo_done["q"], b * 2 + t + 1)
                    if not (isinstance(b, int) and b == 0):
                        wait_apart(sp, sc_made, unit_of(b, (g + 1) * KC, 0) - UNITS)
                    for n, parts in (("q", (hi, lo, hi, lo)), ("k", (hi, hi, lo, lo))):
                        for k, part in enumerate(parts):
                            for j in range(HG):
                                r0 = (half * HG + j) * D
                                sp.dma_start(stack[n][k * D:(k + 1) * D, g * HG + j, :].bitcast(F32),
                                             part[n][r0:r0 + D, t, :].bitcast(F32)
                                             ).then_inc(stacked[g], DMA)

                def place_max(b, g):
                    wait_apart(sp, mlo_done, b * NG + g + 1)
                    for k, part in enumerate((m_hi, m_lo)):
                        dst = stack["q"][MROW + k:MROW + k + 1, g * HG:(g + 1) * HG, :].bitcast(F32)
                        sp.dma_start(dst.rearrange("o h (c n) -> o (h c) n", n=P),
                                     part[:, :].bitcast(F32)).then_inc(m_placed[g], DMA)

                def place_ctx(b, g):
                    wait_apart(sp, pv_out, b * NG + g + 1)
                    if not (isinstance(b, int) and b == 0):
                        wait_apart(sp, wo_made, b * CT)
                    for dst, r0 in ((ctx_raw, 0), (row_sum, D)):
                        for j in range(HG):
                            at, fr = (g % GPT * HG + j) * D, j * 2 * D + r0
                            sp.dma_start(dst[at:at + D, g // GPT, :], pv_sb[fr:fr + D, g % 2, :]
                                         ).then_inc(ctx_placed[g], DMA)

                def store_r(b):
                    wait_apart(sp, r_done, b * CT + CT)
                    sp.dma_start(r_dram[b].rearrange("(t p) n -> p t n", p=P), r_out[:, :, :]
                                 ).then_inc(r_stored, DMA)

                def keep_q(b):
                    wait_apart(sp, ln_done["q"], b * 2 + 2)
                    if not (isinstance(b, int) and b == 0):
                        wait_apart(sp, r_done, b * CT)
                    sp.dma_start(q_res[:, :, :], ln["q"][:, :, :]).then_inc(q_kept, DMA)

                def batch(b, first=False, last=False, load_more=True):
                    fill_stack(b, NG - 1)
                    if not first:
                        place_ctx(b - 1, NG - 1)
                    if load_more:
                        load(b + 2, "k")
                        load(b + 2, "q")
                    place_max(b, 1)
                    place_ctx(b, 0)
                    if not first:
                        store_r(b - 1)
                    keep_q(b)
                    place_max(b, 2)
                    if not last:
                        fill_stack(b + 1, 0)
                        fill_stack(b + 1, 1)
                    place_ctx(b, 1)
                    place_max(b, 3)
                    if not last:
                        fill_stack(b + 1, 2)
                    place_ctx(b, 2)
                    if not last:
                        place_max(b + 1, 0)

                load(0, "k")
                sp.dma_start(pe_tab[:, :, :], pos.rearrange("(t p) n -> p t n", p=P)).then_inc(weights, DMA)
                load(0, "q")
                load(1, "k")
                load(1, "q")
                for g in range(NG - 1):
                    fill_stack(0, g)
                place_max(0, 0)
                batch(0, first=True)
                with sp.Fori(1, B - 2) as b:
                    batch(b)
                batch(B - 2, load_more=False)
                batch(B - 1, last=True, load_more=False)
                place_ctx(B - 1, NG - 1)
                store_r(B - 1)
                sp.wait_ge(r_stored, B * DMA)

            @block.gpsimd
            def _(pool):
                def add_pos(b, n):
                    pool.wait_ge(loaded[n], b * DMA + DMA)
                    pool.tensor_tensor(src[n][:, :, :], src[n][:, :, :], pe_tab[:, :, :], ALU.add
                                       ).then_inc(pos_added[n], 1)

                def normalise(b, n):
                    wait_apart(pool, stat_done[n], b * KC + KC)
                    pool.tensor_scalar(rstd[n][:, :], mv[n][:, :, 1], EPS, None, ALU.add
                                       ).then_inc(rstd_step[n], 1)
                    pool.wait_ge(rstd_step[n], b * 2 + 1)
                    pool.tensor_tensor(rstd[n][:, :], rstd[n][:, :], neg_half[:, :], ALU.pow
                                       ).then_inc(rstd_step[n], 1)
                    wait_apart(pool, rstd_step[n], b * 2 + 2)
                    for c in range(KC):
                        pool.tensor_scalar(tok[n][:, c, :], tok[n][:, c, :], mv[n][:, c, 0:1],
                                           rstd[n][:, c:c + 1], ALU.subtract, ALU.mult
                                           ).then_inc(normed[n], 1)

                def batch(b, last=False, load_more=True):
                    if not last:
                        normalise(b + 1, "k")
                        normalise(b + 1, "q")
                    if load_more:
                        add_pos(b + 2, "k")
                        add_pos(b + 2, "q")

                pool.memset(ident[:, :], 0.0).then_inc(consts, 1)
                pool.memset(neg_half[:, :], -0.5).then_inc(consts, 1)
                pool.wait_ge(consts, 2)
                pool.affine_select(out=ident[:, :], in_=ident[:, :], compare_op=ALU.not_equal, fill=1.0,
                                   base=0, pattern=[[-1, P]], channel_multiplier=1).then_inc(consts, 1)
                pool.wait_ge(consts, 3)
                pool.memset(stack["q"][ZROW:MROW + 2, :, :].bitcast(F32), 0.0).then_inc(consts, 1)
                pool.wait_ge(consts, 4)
                pool.memset(stack["k"][ZROW:MROW + 2, :, :].bitcast(F32), 1.0).then_inc(consts, 1)
                pool.wait_ge(consts, 5)
                pool.wait_ge(weights, 12 * DMA)
                add_pos(0, "k")
                add_pos(0, "q")
                pool.memset(v_ones[:, :, :, D:2 * D], 1.0).then_inc(consts, 1)
                normalise(0, "k")
                normalise(0, "q")
                add_pos(1, "k")
                add_pos(1, "q")
                batch(0)
                with pool.Fori(1, B - 2) as b:
                    batch(b)
                batch(B - 2, load_more=False)
                batch(B - 1, last=True, load_more=False)

            @block.scalar
            def _(act):
                def take_tok(b, n, half):
                    act.wait_ge(tr_in[n], b * 2 + half + 1)
                    if half == 0 and not (isinstance(b, int) and b == 0):
                        act.wait_ge(tr_out[n], b * 2)
                    act.activation(tok[n][:, 2 * half:2 * half + 2, :], tr_ps[:, :], ACT.Copy
                                   ).then_inc(tok_ready[n], 1)

                def take_ln(b, n, t):
                    act.wait_ge(tr_out[n], b * 2 + t + 1)
                    if t == 0 and not (isinstance(b, int) and b == 0):
                        act.wait_ge(proj[n], b * 2)
                        if n == "k":
                            act.wait_ge(v_made, b * KC)
                        else:
                            act.wait_ge(q_kept, b * DMA)
                    act.activation(ln[n][:, t, :], tr_ps[:, :], ACT.Identity,
                                   scale=gain[n][:, t:t + 1], bias=bias[n][:, t:t + 1]
                                   ).then_inc(ln_done[n], 1)

                def take_hi(b, n, t):
                    act.wait_ge(proj[n], b * 2 + t + 1)
                    if not (isinstance(b, int) and b == 0):
                        for g in range(t * GPT, (t + 1) * GPT):
                            act.wait_ge(stacked[g], b * STACK)
                    act.activation(hi[n][:, t, :], pj_ps[:, :], ACT.Copy).then_inc(hi_done[n], 1)

                def take_v(b, c):
                    act.wait_ge(v_made, b * KC + c + 1)
                    if not (isinstance(b, int) and b == 0):
                        act.wait_ge(pv_made, b * STEPS + c + 1 - KC)
                    act.activation(v_ones[:, c, :, 0:D],
                                   xc_ps[:, 0:C].rearrange("p (h d) -> p h d", d=D), ACT.Copy
                                   ).then_inc(v_done, 1)

                def exp(b, s, j, first=False):
                    act.wait_ge(sc_made, unit_of(b, s, j) + 1)
                    if j == 0 and not (first and s < 2):
                        act.wait_ge(pv_made, b * STEPS + s - 1)
                    act.activation(probs[:, s % 2, j, :], sc_ps[j % 2][:, :], ACT.Exp, scale=SCALE
                                   ).then_inc(exp_done, 1)

                def take_pv(b, g, first=False):
                    act.wait_ge(pv_made, b * STEPS + (g + 1) * KC)
                    if g >= 2:
                        act.wait_ge(ctx_placed[g - 2], b * PLACED + PLACED)
                    elif not first:
                        act.wait_ge(ctx_placed[g + 2], b * PLACED)
                    act.activation(pv_sb[:, g % 2, :], pv_ps[:, :], ACT.Copy).then_inc(pv_out, 1)

                def batch(b, first=False, last=False):
                    for s in range(STEPS):
                        exp(b, s, 0, first)
                        exp(b, s, 1, first)
                        if s == 1:
                            take_v(b, 3)
                        if s == 1 and not last:
                            take_tok(b + 1, "k", 1)
                        if s == 2 and not last:
                            take_tok(b + 1, "q", 1)
                        if s == 5 and not last:
                            take_ln(b + 1, "k", 1)
                        if s == 6 and not last:
                            take_hi(b + 1, "k", 0)
                        if s == 7 and not last:
                            take_ln(b + 1, "q", 1)
                            take_hi(b + 1, "k", 1)
                        if s in (8, 9) and not last:
                            take_hi(b + 1, "q", s - 8)
                        if s == 14 and not last:
                            take_v(b + 1, 0)
                        if s == 15 and not last:
                            take_v(b + 1, 1)
                        if s == 0 and not first:
                            take_v(b, 2)
                        exp(b, s, 2, first)
                        exp(b, s, 3, first)
                        if s % KC == 0 and s:
                            take_pv(b, s // KC - 1, first)
                        if s == 0 and not first:
                            take_pv(b - 1, NG - 1)
                        if last:
                            continue
                        if s == 0:
                            take_tok(b + 1, "k", 0)
                        if s == 1:
                            take_tok(b + 1, "q", 0)
                        if s == 4:
                            take_ln(b + 1, "k", 0)
                        if s == 6:
                            take_ln(b + 1, "q", 0)

                act.dma_start(w_k[:, :, :], Wk.rearrange("(t p) n -> p t n", p=P)).then_inc(weights, DMA)
                act.dma_start(w_q[:, :, :], Wq.rearrange("(t p) n -> p t n", p=P)).then_inc(weights, DMA)
                act.dma_start(w_v[:, :, :], Wv.rearrange("(t p) n -> p t n", p=P)).then_inc(weights, DMA)
                act.dma_start(w_o[:, :, :], Wo.rearrange("(t p) n -> p t n", p=P)).then_inc(weights, DMA)
                for dst, v in ((gq, ln_q_g), (bq, ln_q_b), (gk, ln_kv_g), (bk, ln_kv_b),
                               (gf, ffn_g), (bf, ffn_b), (b2_col, b2)):
                    act.dma_start(dst, v.rearrange("(t p) -> p t", p=P),
                                  allow_slow_non_contiguous=True).then_inc(weights, DMA)
                act.wait_ge(weights, 12 * DMA)
                for n in "kq":
                    for half in range(2):
                        take_tok(0, n, half)
                for n in "kq":
                    for t in range(CT):
                        take_ln(0, n, t)
                for t in range(CT):
                    for n in "kq":
                        take_hi(0, n, t)
                for c in range(3):
                    take_v(0, c)
                batch(0, first=True)
                with act.Fori(1, B - 1) as b:
                    batch(b)
                batch(B - 1, last=True)
                take_pv(B - 1, NG - 1)

            @block.vector
            def _(dve):
                def stats(b, n):
                    for c in range(KC):
                        dve.wait_ge(tok_ready[n], b * 2 + c // 2 + 1)
                        dve.bn_stats(stat[n][:, c, :], tok[n][:, c, :]).then_inc(bn_done[n], 1)
                    if not (isinstance(b, int) and b == 0):
                        wait_apart(dve, normed[n], b * KC)
                    for c in range(KC):
                        wait_apart(dve, bn_done[n], b * KC + c + 1)
                        dve.bn_aggr(mv[n][:, c, :], stat[n][:, c, :]).then_inc(stat_done[n], 1)

                def take_lo(b, n, t):
                    dve.wait_ge(hi_done[n], b * 2 + t + 1)
                    dve.tensor_tensor(lo[n][:, t, :], pj_ps[:, :], hi[n][:, t, :].bitcast(F32),
                                      ALU.subtract).then_inc(lo_done[n], 1)

                def row_max(b, q, j, first=False):
                    g, c = q // KC, q % KC
                    dve.wait_ge(mx_made, unit_of(b, q, j) + 1)
                    if c == 0 and j == 0 and not (first and g < 2):
                        dve.wait_ge(mt_made, b * NG + g - 1)
                    dve.tensor_reduce(neg_max[:, g % 2, j * KC + c:j * KC + c + 1], mx_ps[j % 2][:, :],
                                      AX_X, ALU.max, negate=True).then_inc(mx_done, 1)

                def split_max(b, g, first=False):
                    dve.wait_ge(mt_made, b * NG + g + 1)
                    if g >= 1:
                        dve.wait_ge(m_placed[g - 1], b * 2 * DMA + 2 * DMA)
                    elif not first:
                        dve.wait_ge(m_placed[NG - 1], b * 2 * DMA)
                    dve.tensor_copy(m_hi[:, :], xc_ps[0:HG * KC, 0:P]).then_inc(mhi_done, 1)
                    dve.wait_ge(mhi_done, b * NG + g + 1)
                    dve.tensor_tensor(m_lo[:, :], xc_ps[0:HG * KC, 0:P], m_hi[:, :].bitcast(F32),
                                      ALU.subtract).then_inc(mlo_done, 1)

                def invert_sums(b, t, c):
                    if c == 0:
                        for g in range(t * GPT, (t + 1) * GPT):
                            dve.wait_ge(ctx_placed[g], b * PLACED + PLACED)
                    part = row_sum[:, t, c * P:(c + 1) * P]
                    dve.reciprocal(part, part).then_inc(inverted, 1)

                def scale_ctx(b, t):
                    dve.wait_ge(inverted, (b * CT + t + 1) * KC)
                    dve.tensor_tensor(ctx_raw[:, t, :], ctx_raw[:, t, :], row_sum[:, t, :], ALU.mult
                                      ).then_inc(ctx_done, 1)

                def add_q(b, t):
                    dve.wait_ge(wo_made, b * CT + t + 1)
                    if t == 0:
                        dve.wait_ge(q_kept, b * DMA + DMA)
                        if not (isinstance(b, int) and b == 0):
                            dve.wait_ge(r_stored, b * DMA)
                    dve.tensor_tensor(r_out[:, t, :], xc_ps[:, :], q_res[:, t, :], ALU.add
                                      ).then_inc(r_done, 1)

                def batch(b, first=False, last=False):
                    for s in range(STEPS):
                        q = s + LEAD
                        nb, nq = (b, q) if q < STEPS else (b + 1, q - STEPS)
                        todo = q < STEPS or not last
                        if todo:
                            row_max(nb, nq, 0, first and q < STEPS)
                            row_max(nb, nq, 1, first and q < STEPS)
                        if s == 1 and not last:
                            stats(b + 1, "k")
                        if s == 2 and not last:
                            stats(b + 1, "q")
                        if s == 2 and not first:
                            invert_sums(b - 1, 1, 1)
                        if s == 3 and not first:
                            invert_sums(b - 1, 1, 3)
                            scale_ctx(b - 1, 1)
                        if s == 5 and not first:
                            add_q(b - 1, 1)
                        if s in (6, 7) and not last:
                            take_lo(b + 1, "k", s - 6)
                        if s in (8, 9) and not last:
                            take_lo(b + 1, "q", s - 8)
                        if s in (11, 12):
                            invert_sums(b, 0, 2 * (s - 11))
                        if todo:
                            row_max(nb, nq, 2, first and q < STEPS)
                            row_max(nb, nq, 3, first and q < STEPS)
                        if s % KC == KC - 1 and s + 1 < STEPS:
                            split_max(b, (s + 1) // KC)
                        if s == STEPS - 1 and not last:
                            split_max(b + 1, 0)
                        if s in (1, 2) and not first:
                            invert_sums(b - 1, 1, 2 * (s - 1))
                        if s == 4 and not first:
                            add_q(b - 1, 0)
                        if s in (11, 12):
                            invert_sums(b, 0, 2 * (s - 11) + 1)
                        if s == 12:
                            scale_ctx(b, 0)

                stats(0, "k")
                stats(0, "q")
                for t in range(CT):
                    for n in "kq":
                        take_lo(0, n, t)
                for q in range(LEAD):
                    for j in range(HG):
                        row_max(0, q, j, True)
                    if q == KC - 1:
                        split_max(0, 0, True)
                batch(0, first=True)
                with dve.Fori(1, B - 1) as b:
                    batch(b)
                batch(B - 1, last=True)
                for c in range(KC):
                    invert_sums(B - 1, 1, c)
                scale_ctx(B - 1, 1)
                for t in range(CT):
                    add_q(B - 1, t)

            @block.tensor
            def _(pe):
                def transpose_in(b, n, half):
                    if half == 0:
                        pe.wait_ge(pos_added[n], b + 1)
                    if half == 1:
                        pe.wait_ge(tok_ready[n], b * 2 + 1)
                    elif n == "q":
                        pe.wait_ge(tok_ready["k"], b * 2 + 2)
                    elif not (isinstance(b, int) and b == 0):
                        pe.wait_ge(ln_done["q"], b * 2)
                    for c in range(2):
                        for t in range(CT):
                            at = c * C + t * P
                            m = pe.transpose(tr_ps[:, at:at + P],
                                             src[n][:, t, (2 * half + c) * P:(2 * half + c + 1) * P],
                                             ident[:, :])
                    m.then_inc(tr_in[n], 1)

                def transpose_out(b, n, t):
                    if t == 0:
                        pe.wait_ge(normed[n], b * KC + KC)
                    if t == 1:
                        pe.wait_ge(ln_done[n], b * 2 + 1)
                    elif n == "k":
                        pe.wait_ge(tok_ready["q"], b * 2 + 2)
                    else:
                        pe.wait_ge(ln_done["k"], b * 2 + 2)
                    for c in range(KC):
                        m = pe.transpose(tr_ps[:, c * P:(c + 1) * P], tok[n][:, c, t * P:(t + 1) * P],
                                         ident[:, :])
                    m.then_inc(tr_out[n], 1)

                def project(b, n, t):
                    if t == 0:
                        pe.wait_ge(ln_done[n], b * 2 + 2)
                    if isinstance(b, int) and b == 0:
                        if n == "q":
                            pe.wait_ge(lo_done["k"], t + 1)
                        elif t == 1:
                            pe.wait_ge(lo_done["q"], 1)
                    elif t == 1:
                        pe.wait_ge(lo_done[n], b * 2 + 1)
                    elif n == "q":
                        pe.wait_ge(lo_done["k"], b * 2 + 2)
                    else:
                        pe.wait_ge(lo_done["q"], b * 2)
                    for k in range(CT):
                        m = pe.matmul(pj_ps[:, :], w_of[n][:, k, t * P:(t + 1) * P], ln[n][:, k, :],
                                      start=(k == 0), stop=(k == CT - 1))
                    m.then_inc(proj[n], 1)

                def make_v(b, c):
                    if c == 0:
                        pe.wait_ge(ln_done["k"], b * 2 + 2)
                        if not (isinstance(b, int) and b == 0):
                            pe.wait_ge(mlo_done, b * NG)
                    elif c == 2 and not (isinstance(b, int) and b == 0):
                        pe.wait_ge(mlo_done, b * NG + 1)
                    elif c == 3 and isinstance(b, int) and b == 0:
                        pe.wait_ge(mlo_done, 1)
                    else:
                        pe.wait_ge(v_done, b * KC + c)
                    for k in range(CT):
                        m = pe.matmul(xc_ps[:, 0:C], ln["k"][:, k, c * P:(c + 1) * P], w_v[:, k, :],
                                      start=(k == 0), stop=(k == CT - 1))
                    m.then_inc(v_made, 1)

                def transpose_max(b, g, first=False, last=False):
                    pe.wait_ge(mx_done, unit_of(b, (g + 1) * KC, 0))
                    if g == 0:
                        pe.wait_ge(v_done, b * KC + (3 if first else 2))
                    elif g == 1:
                        pe.wait_ge(v_done, b * KC + KC)
                    elif g == 2 and not first:
                        pe.wait_ge(r_done, b * CT)
                    else:
                        pe.wait_ge(mlo_done, b * NG + g)
                    pe.transpose(xc_ps[0:HG * KC, 0:P], neg_max[:, g % 2, :], ident[:, :]
                                 ).then_inc(mt_made, 1)

                def max_scores(b, q, j, fresh=False):
                    g, c = q // KC, q % KC
                    if c == 0 and j == 0:
                        pe.wait_ge(stacked[g], b * STACK + STACK)
                    if not (fresh and q == 0 and j < 2):
                        pe.wait_ge(mx_done, unit_of(b, q, j) - 1)
                    h = g * HG + j
                    pe.matmul(mx_ps[j % 2][:, :], stack["q"][0:MROW, h, c * P:(c + 1) * P],
                              stack["k"][0:MROW, h, :], start=True, stop=True).then_inc(mx_made, 1)

                def scores(b, s, j, first=False):
                    g, c = s // KC, s % KC
                    if c == 0 and j == 0:
                        pe.wait_ge(m_placed[g], b * 2 * DMA + 2 * DMA)
                    if not (first and s == 0 and j < 2):
                        pe.wait_ge(exp_done, unit_of(b, s, j) - 1)
                    h = g * HG + j
                    pe.matmul(sc_ps[j % 2][:, :], stack["k"][0:MROW + 2, h, c * P:(c + 1) * P],
                              stack["q"][0:MROW + 2, h, :], start=True, stop=True).then_inc(sc_made, 1)

                def prob_value(b, s, first=False):
                    g, c = s // KC, s % KC
                    pe.wait_ge(exp_done, unit_of(b, s + 1, 0))
                    pe.wait_ge(v_done, b * KC + c + 1)
                    if c == 0 and not (first and g == 0):
                        pe.wait_ge(pv_out, b * NG + g)
                    for j in range(HG):
                        m = pe.matmul(pv_ps[32 * j:32 * j + 32, :], v_ones[:, c, g * HG + j, :],
                                      probs[:, s % 2, j, :], start=(c == 0), stop=(c == KC - 1))
                    m.then_inc(pv_made, 1)

                def out_proj(b, t, b_next=True):
                    if t == 0:
                        pe.wait_ge(ctx_done, b * CT + CT)
                        pe.wait_ge(mlo_done, b * NG + NG + (2 if b_next else 0))
                    else:
                        pe.wait_ge(r_done, b * CT + 1)
                    for k in range(CT):
                        m = pe.matmul(xc_ps[:, :], w_o[:, k, t * P:(t + 1) * P], ctx_raw[:, k, :],
                                      start=(k == 0), stop=(k == CT - 1))
                    m.then_inc(wo_made, 1)

                def batch(b, first=False, last=False):
                    for s in range(STEPS):
                        q = s + LEAD
                        nb, nq = (b, q) if q < STEPS else (b + 1, q - STEPS)
                        todo = q < STEPS or not last
                        for j in (0, 1):
                            scores(b, s, j, first)
                            if todo:
                                max_scores(nb, nq, j)
                        if s % KC == KC - 1:
                            if s + 1 < STEPS:
                                transpose_max(b, (s + 1) // KC, first)
                            elif not last:
                                transpose_max(b + 1, 0)
                        if s:
                            prob_value(b, s - 1, first)
                        elif not first:
                            prob_value(b - 1, STEPS - 1)
                        if s == 4 and not first:
                            out_proj(b - 1, 0)
                        if not last:
                            if s == 0:
                                transpose_in(b + 1, "k", 0)
                            if s == 1:
                                transpose_in(b + 1, "q", 0)
                            if s == 4:
                                transpose_out(b + 1, "k", 0)
                            if s == 6:
                                transpose_out(b + 1, "q", 0)
                        for j in (2, 3):
                            scores(b, s, j, first)
                            if todo:
                                max_scores(nb, nq, j)
                        if s == 0:
                            make_v(b, 3)
                        if s == 4 and not first:
                            out_proj(b - 1, 1)
                        if last:
                            continue
                        if s == 0:
                            transpose_in(b + 1, "k", 1)
                        if s == 1:
                            transpose_in(b + 1, "q", 1)
                        if s == 4:
                            transpose_out(b + 1, "k", 1)
                        if s == 6:
                            transpose_out(b + 1, "q", 1)
                        if s in (5, 6):
                            project(b + 1, "k", s - 5)
                        if s in (7, 8):
                            project(b + 1, "q", s - 7)
                        if s in (13, 14, 15):
                            make_v(b + 1, s - 13)

                pe.wait_ge(consts, 6)
                pe.wait_ge(weights, 12 * DMA)
                for n in "kq":
                    for half in range(2):
                        transpose_in(0, n, half)
                for n in "kq":
                    for t in range(CT):
                        transpose_out(0, n, t)
                for t in range(CT):
                    for n in "kq":
                        project(0, n, t)
                for c in range(3):
                    make_v(0, c)
                for q in range(LEAD):
                    for j in range(HG):
                        max_scores(0, q, j, fresh=True)
                    if q == KC - 1:
                        transpose_max(0, 0, first=True)
                batch(0, first=True)
                with pe.Fori(1, B - 1) as b:
                    batch(b)
                batch(B - 1, last=True)
                prob_value(B - 1, STEPS - 1)
                for t in range(CT):
                    out_proj(B - 1, t, b_next=False)

        r_buf = sb("r_buf", [P, 2, CT, T])
        h_buf = sb("h_buf", [P, 2, CT, T])
        act_buf = sb("act_buf", [P, FT, T])
        tok_f = tok["k"]
        out_buf = x_in
        stat_f, mv_f, rstd_f = stat["k"], mv["k"], rstd["k"]
        up_ps, down_ps = sc_ps + mx_ps, [pv_ps, pj_ps]
        t_ps = [tr_ps, xc_ps]

        ffw_weights = sem("ffw_weights")
        r_loaded = [sem("r_loaded0"), sem("r_loaded1")]
        f_tr_in = sem("f_tr_in")
        f_tok = sem("f_tok")
        f_bn = sem("f_bn")
        f_stat = sem("f_stat")
        f_rstd = sem("f_rstd")
        f_normed = sem("f_normed")
        f_tr_out = sem("f_tr_out")
        f_ln = sem("f_ln")
        up_made = sem("up_made")
        gelu_done = sem("gelu_done")
        down_made = sem("down_made")
        out_done = sem("out_done")
        out_stored = sem("out_stored")

        with nc.Block() as block:
            def zero(b):
                return isinstance(b, int) and b == 0

            def pairs(eng, batch):
                batch(0, 0)
                batch(1, 1)
                with eng.Fori(1, B // 2 - 1) as i:
                    batch(2 * i, 0)
                    batch(2 * i + 1, 1)
                batch(B - 2, 0)
                batch(B - 1, 1, last=True)

            @block.sync
            def _(sp):
                def load_r(b, i):
                    if not (isinstance(b, int) and b < 2):
                        wait_apart(sp, out_done, b * CT - 2 * CT)
                    sp.dma_start(r_buf[:, i, :, :], r_dram[b].rearrange("(t p) n -> p t n", p=P)
                                 ).then_inc(r_loaded[i], DMA)

                def store(b):
                    wait_apart(sp, out_done, b * CT + CT)
                    sp.dma_start(out[b].rearrange("(t p) n -> p t n", p=P), out_buf[:, :, :]
                                 ).then_inc(out_stored, DMA)

                load_r(0, 0)
                sp.dma_start(w_1[:, :, :], W1.rearrange("(t p) n -> p t n", p=P)).then_inc(ffw_weights, DMA)
                sp.dma_start(w_2[:, :, :], W2.rearrange("(t p) n -> p t n", p=P)).then_inc(ffw_weights, DMA)
                sp.dma_start(b1_col[:, :], b1.rearrange("(t p) -> p t", p=P),
                             allow_slow_non_contiguous=True).then_inc(ffw_weights, DMA)
                load_r(1, 1)
                with sp.Fori(0, B // 2 - 1) as i:
                    store(2 * i)
                    load_r(2 * i + 2, 0)
                    store(2 * i + 1)
                    load_r(2 * i + 3, 1)
                store(B - 2)
                store(B - 1)
                sp.wait_ge(out_stored, B * DMA)

            @block.gpsimd
            def _(pool):
                def inv_std(b):
                    wait_apart(pool, f_stat, b * KC + KC)
                    if not zero(b):
                        pool.wait_ge(f_normed, b * KC)
                    pool.tensor_scalar(rstd_f[:, :], mv_f[:, :, 1], EPS, None, ALU.add).then_inc(f_rstd, 1)
                    pool.wait_ge(f_rstd, b * 2 + 1)
                    pool.tensor_tensor(rstd_f[:, :], rstd_f[:, :], neg_half[:, :], ALU.pow
                                       ).then_inc(f_rstd, 1)

                inv_std(0)
                with pool.Fori(1, B) as b:
                    inv_std(b)

            @block.scalar
            def _(act):
                def take_tok(b, half):
                    act.wait_ge(f_tr_in, b * 2 + half + 1)
                    if half == 0 and not zero(b):
                        act.wait_ge(f_tr_out, b * 2)
                    act.activation(tok_f[:, 2 * half:2 * half + 2, :], t_ps[half][:, :], ACT.Copy
                                   ).then_inc(f_tok, 1)

                def take_ln(b, i, t):
                    act.wait_ge(f_tr_out, b * 2 + t + 1)
                    if not (isinstance(b, int) and b < 2):
                        act.wait_ge(up_made, b * FT - FT)
                    act.activation(h_buf[:, i, t, :], t_ps[t][:, :], ACT.Identity,
                                   scale=gf[:, t:t + 1], bias=bf[:, t:t + 1]).then_inc(f_ln, 1)

                def gelu(b, f):
                    act.wait_ge(up_made, b * FT + f + 1)
                    if f == 0 and not zero(b):
                        act.wait_ge(down_made, b * CT)
                    act.activation(act_buf[:, f, :], up_ps[f][:, :], ACT.Gelu,
                                   bias=b1_col[:, f:f + 1]).then_inc(gelu_done, 1)

                def batch(b, i, last=False):
                    if not last:
                        take_tok(b + 1, 0)
                        take_tok(b + 1, 1)
                    for f in range(FT):
                        gelu(b, f)
                    if not last:
                        take_ln(b + 1, 1 - i, 0)
                        take_ln(b + 1, 1 - i, 1)

                act.wait_ge(ffw_weights, 3 * DMA)
                take_tok(0, 0)
                take_tok(0, 1)
                take_ln(0, 0, 0)
                take_ln(0, 0, 1)
                pairs(act, batch)

            @block.vector
            def _(dve):
                def normalise(b):
                    for c in range(KC):
                        dve.wait_ge(f_tok, b * 2 + c // 2 + 1)
                        dve.bn_stats(stat_f[:, c, :], tok_f[:, c, :]).then_inc(f_bn, 1)
                    for c in range(KC):
                        wait_apart(dve, f_bn, b * KC + c + 1)
                        dve.bn_aggr(mv_f[:, c, :], stat_f[:, c, :]).then_inc(f_stat, 1)
                    dve.wait_ge(f_rstd, b * 2 + 2)
                    for c in range(KC):
                        dve.tensor_scalar(tok_f[:, c, :], tok_f[:, c, :], mv_f[:, c, 0:1],
                                          rstd_f[:, c:c + 1], ALU.subtract, ALU.mult
                                          ).then_inc(f_normed, 1)

                def finish(b, i, t):
                    dve.wait_ge(down_made, b * CT + t + 1)
                    if t == 0 and not zero(b):
                        dve.wait_ge(out_stored, b * DMA)
                    if t == 0:
                        dve.wait_ge(ffw_weights, 3 * DMA)
                    dve.scalar_tensor_tensor(out_buf[:, t, :], down_ps[t][:, :], b2_col[:, t:t + 1],
                                             r_buf[:, i, t, :], ALU.add, ALU.add).then_inc(out_done, 1)

                def batch(b, i, last=False):
                    if not last:
                        normalise(b + 1)
                    finish(b, i, 0)
                    finish(b, i, 1)

                normalise(0)
                pairs(dve, batch)

            @block.tensor
            def _(pe):
                def transpose_in(b, i, half):
                    if half == 0:
                        pe.wait_ge(r_loaded[i], (b - i) * (DMA // 2) + DMA)
                        if not zero(b):
                            pe.wait_ge(f_ln, b * 2)
                    for c in range(2):
                        for t in range(CT):
                            at = c * C + t * P
                            m = pe.transpose(t_ps[half][:, at:at + P],
                                             r_buf[:, i, t, (2 * half + c) * P:(2 * half + c + 1) * P],
                                             ident[:, :])
                    m.then_inc(f_tr_in, 1)

                def transpose_out(b, t):
                    if t == 0:
                        pe.wait_ge(f_normed, b * KC + KC)
                        pe.wait_ge(f_tok, b * 2 + 2)
                    for c in range(KC):
                        m = pe.transpose(t_ps[t][:, c * P:(c + 1) * P], tok_f[:, c, t * P:(t + 1) * P],
                                         ident[:, :])
                    m.then_inc(f_tr_out, 1)

                def up(b, i, f):
                    if f == 0:
                        pe.wait_ge(f_ln, b * 2 + 2)
                    if not zero(b):
                        pe.wait_ge(gelu_done, b * FT - FT + f + 1)
                    for k in range(CT):
                        m = pe.matmul(up_ps[f][:, :], w_1[:, k, f * P:(f + 1) * P], h_buf[:, i, k, :],
                                      start=(k == 0), stop=(k == CT - 1))
                    m.then_inc(up_made, 1)

                def down(b, t):
                    if not zero(b):
                        pe.wait_ge(out_done, b * CT - CT + t + 1)
                    for f in range(FT):
                        if t == 0:
                            pe.wait_ge(gelu_done, b * FT + f + 1)
                        m = pe.matmul(down_ps[t][:, :], w_2[:, f, t * P:(t + 1) * P], act_buf[:, f, :],
                                      start=(f == 0), stop=(f == FT - 1))
                    m.then_inc(down_made, 1)

                def batch(b, i, last=False):
                    if not last:
                        transpose_in(b + 1, 1 - i, 0)
                        transpose_in(b + 1, 1 - i, 1)
                    for f in range(FT):
                        up(b, i, f)
                    if not last:
                        transpose_out(b + 1, 0)
                        transpose_out(b + 1, 1)
                    down(b, 0)
                    down(b, 1)

                pe.wait_ge(ffw_weights, 3 * DMA)
                transpose_in(0, 0, 0)
                transpose_in(0, 0, 1)
                transpose_out(0, 0)
                transpose_out(0, 1)
                pairs(pe, batch)


_INS = ['x', 'ctx_2048', 'L0_xattn_Wq', 'L0_xattn_Wk', 'L0_xattn_Wv', 'L0_xattn_Wo', 'L0_xattn_ln_q_g',
        'L0_xattn_ln_q_b', 'L0_xattn_ln_kv_g', 'L0_xattn_ln_kv_b', 'L0_xattn_ffn_ln_g', 'L0_xattn_ffn_ln_b',
        'L0_xattn_W1', 'L0_xattn_b1', 'L0_xattn_W2', 'L0_xattn_b2']
_OUTS = [((16, 256, 512), 'float32')]


def positions(c, t):
    import math
    import numpy as np
    f = np.float32
    div = np.exp((np.arange(0, c, 2, dtype=f) * f(-math.log(10000.0) / c)).astype(np.float64)).astype(f)
    ang = (np.arange(t, dtype=f)[:, None] * div).astype(np.float64)
    pe = np.zeros((t, c), f)
    pe[:, 0::2] = np.sin(ang)
    pe[:, 1::2] = np.cos(ang)
    return np.ascontiguousarray(pe.T)


def kernel(**inputs):
    import numpy as _np
    import concourse.bacc as _bacc
    from concourse import mybir as _mybir
    from concourse.bass_utils import run_bass_kernel_spmd as _run

    nc = _bacc.Bacc("TRN2", target_bir_lowering=False, num_devices=1)
    arrays, args = {}, []
    for name in _INS:
        a = _np.ascontiguousarray(inputs[name])
        arrays[f"in_{name}_dram"] = a
        args.append(nc.dram_tensor(f"in_{name}_dram", a.shape, _mybir.dt.from_np(a.dtype), kind="ExternalInput").ap())
    table = positions(inputs["x"].shape[1], inputs["x"].shape[2])
    arrays["in_positions_dram"] = table
    args.append(nc.dram_tensor("in_positions_dram", table.shape, _mybir.dt.from_np(table.dtype), kind="ExternalInput").ap())
    for i, (shape, dtype) in enumerate(_OUTS):
        dt = _mybir.dt.from_np(_np.dtype(dtype))
        args.append(nc.dram_tensor(f"out_{i}_dram", shape, dt, kind="ExternalOutput").ap())
    xattn_kernel(nc, *args)
    r = _run(nc, [arrays], core_ids=[0])
    return r.results[0]["out_0_dram"]
```

```python
from contextlib import ExitStack

import concourse.bass as bass
from concourse import mybir

F32 = mybir.dt.float32
F32R = mybir.dt.float32r
ALU = mybir.AluOpType
ACT = mybir.ActivationFunctionType
AX_X = mybir.AxisListType.X

P = 128
D = 16
HG = 4
EPS = 1e-5
TERMS = 4
ZROW = TERMS * D
MROW = P - 2
ONES = 96
DMA = 16


def xattn_kernel(nc, x, ctx_in, Wq, Wk, Wv, Wo, ln_q_g, ln_q_b, ln_kv_g, ln_kv_b,
                 ffn_g, ffn_b, W1, b1, W2, b2, pos, out):
    B, C, T = x.shape
    H = C // D
    CT = C // P
    KC = T // P
    NG = H // HG
    STEPS = NG * KC
    UNITS = STEPS * HG
    F = W1.shape[1]
    FT = F // P
    LEAD = KC + 2
    STACK = 2 * TERMS * DMA
    SCALE = float(D) ** -0.5

    HPT = H // CT
    PAIR = HG // CT

    def head(g, j):
        return j % CT * HPT + g * PAIR + j // CT

    r_dram = nc.dram_tensor("r_scratch", [B, C, T], F32, kind="Internal").ap()
    ctx_dram = nc.dram_tensor("ctx_scratch", [B, H, 2 * D, T], F32, kind="Internal").ap()
    inv_dram = nc.dram_tensor("inv_scratch", [B, H, T], F32, kind="Internal").ap()

    with ExitStack() as es:
        def sb(name, shape, dt=F32):
            return es.enter_context(nc.sbuf_tensor(name, shape, dt))

        def bank(name, shape=(P, 512)):
            return es.enter_context(nc.psum_tensor(name, list(shape), F32))

        def sem(name):
            return es.enter_context(nc.semaphore(name))

        ident = sb("ident", [P, P])
        neg_half = sb("neg_half", [P, KC])
        pe_tab = sb("pe_tab", [P, CT, T])
        w_q, w_k, w_v, w_o = (sb(n, [P, CT, C]) for n in ("w_q", "w_k", "w_v", "w_o"))
        w_1 = sb("w_1", [P, CT, F])
        w_2 = sb("w_2", [P, FT, C])
        vecs = sb("vecs", [P, 10 * CT])
        b1_col = sb("b1_col", [P, FT])
        gq, bq, gk, bk, gf, bf, b2_col = (vecs[:, CT * i:CT * i + CT] for i in range(7))

        x_in = sb("x_in", [P, CT, T])
        kv_in = sb("kv_in", [P, CT, T])
        tok = {"k": sb("tok_k", [P, KC, C]), "q": sb("tok_q", [P, KC, C])}
        stat = {"k": sb("stat_k", [P, KC, 6]), "q": sb("stat_q", [P, KC, 6])}
        mv = {"k": sb("mv_k", [P, KC, 2]), "q": sb("mv_q", [P, KC, 2])}
        rstd = {"k": sb("rstd_k", [P, KC]), "q": sb("rstd_q", [P, KC])}
        ln = {"k": sb("ln_k", [P, CT, T]), "q": sb("ln_q", [P, CT, T])}
        parts = sb("parts", [P, 4, CT, T], F32R)
        hi = {"k": parts[:, 0], "q": parts[:, 2]}
        lo = {"k": parts[:, 1], "q": parts[:, 3]}
        stacks = sb("stacks", [P, NG, 2, PAIR, CT, T], F32R)
        v_ones = sb("v_ones", [P, KC, H, 2 * D])
        probs = sb("probs", [P, 2, HG, T])
        neg_max = sb("neg_max", [P, 2, 2, HG * KC])
        m_hi = sb("m_hi", [2 * HG * KC, P], F32R)
        m_both = sb("m_both", [2 * HG * KC, P], F32R)
        lo_rows = sb("lo_rows", [2 * HG * KC, 1])
        pv_sb = sb("pv_sb", [P, 2, T])
        ctx_raw = sb("ctx_raw", [P, CT, T])
        sums = sb("sums", [P, H * T // P])
        inv_sum = sb("inv_sum", [P, CT, T])
        q_mid = sb("q_mid", [P, CT, T])
        q_res = sb("q_res", [P, CT, T])
        r_out = sb("r_out", [P, CT, T])

        sc_ps = [bank("sc_ps0"), bank("sc_ps1")]
        mx_ps = [bank("mx_ps0"), bank("mx_ps1")]
        pv_ps = bank("pv_ps")
        tr_ps = bank("tr_ps")
        pj_ps = bank("pj_ps")
        xc_ps = bank("xc_ps")

        consts = sem("consts")
        weights = sem("weights")
        loaded = {"k": sem("kv_loaded"), "q": sem("x_loaded")}
        pos_added = {"k": sem("kv_pos_added"), "q": sem("x_pos_added")}
        tr_in = {"k": sem("k_tr_in"), "q": sem("q_tr_in")}
        tok_ready = {"k": sem("k_tok"), "q": sem("q_tok")}
        bn_done = {"k": sem("k_bn"), "q": sem("q_bn")}
        stat_done = {"k": sem("k_stat"), "q": sem("q_stat")}
        rstd_step = {"k": sem("k_rstd"), "q": sem("q_rstd")}
        normed = {"k": sem("k_normed"), "q": sem("q_normed")}
        tr_out = {"k": sem("k_tr_out"), "q": sem("q_tr_out")}
        ln_done = {"k": sem("k_ln"), "q": sem("q_ln")}
        proj = {"k": sem("k_proj"), "q": sem("q_proj")}
        hi_done = {"k": sem("k_hi"), "q": sem("q_hi")}
        lo_done = {"k": sem("k_lo"), "q": sem("q_lo")}
        stacked = [sem(f"stacked{g}") for g in range(NG)]
        v_made = sem("v_made")
        v_done = sem("v_done")
        mx_made = sem("mx_made")
        mx_done = sem("mx_done")
        mx_twice = sem("mx_twice")
        mt_made = sem("mt_made")
        mhi_done = sem("mhi_done")
        mlo_done = sem("mlo_done")
        m_placed = [sem(f"m_placed{g}") for g in range(NG)]
        sc_made = sem("sc_made")
        exp_done = sem("exp_done")
        pv_made = sem("pv_made")
        pv_out = sem("pv_out")
        pv_stored = [sem(f"pv_stored{g}") for g in range(NG)]
        sums_loaded = sem("sums_loaded")
        ctx_loaded = sem("ctx_loaded")
        inv_stored = sem("inv_stored")
        inv_loaded = sem("inv_loaded")
        inverted = sem("inverted")
        ctx_done = sem("ctx_done")
        wo_made = sem("wo_made")
        q_saved = sem("q_saved")
        q_kept = sem("q_kept")
        r_done = sem("r_done")
        r_stored = sem("r_stored")

        def wait_apart(eng, semaphore, value):
            if not isinstance(value, int):
                value = eng.to_reg(value)
            eng.wait_ge(consts, 1)
            eng.wait_ge(semaphore, value)

        def unit_of(b, s, j):
            return b * UNITS + s * HG + j

        qk_ps = {"k": pj_ps, "q": tr_ps}
        src = {"k": kv_in, "q": x_in}
        gain, bias = {"k": gk, "q": gq}, {"k": bk, "q": bq}
        w_of = {"k": w_k, "q": w_q}

        with nc.Block() as block:
            @block.sync
            def _(sp):
                def load(b, n):
                    if not (isinstance(b, int) and b == 0):
                        wait_apart(sp, tr_in[n], b * 2)
                    d = {"k": ctx_in, "q": x}[n]
                    sp.dma_start(src[n][:, :, :], d[b].rearrange("(t p) n -> p t n", p=P)
                                 ).then_inc(loaded[n], DMA)

                def fill_stack(b, g):
                    wait_apart(sp, lo_done["k"], b * 2 + 2)
                    wait_apart(sp, lo_done["q"], b * 2 + 2)
                    if not (isinstance(b, int) and b == 0):
                        wait_apart(sp, sc_made, unit_of(b, (g + 1) * KC, 0) - UNITS)
                    for i in range(PAIR):
                        rows = slice((g * PAIR + i) * D, (g * PAIR + i + 1) * D)
                        for kp in range(2):
                            for qp in range(2):
                                to = (2 * kp + qp) * D
                                sp.dma_start(stacks[to:to + D, g, :, i, :, :].bitcast(F32),
                                             parts[rows, kp:qp + 3:qp + 2 - kp, :, :].bitcast(F32)
                                             ).then_inc(stacked[g], DMA)

                def store_pv(b, g):
                    wait_apart(sp, pv_out, b * NG + g + 1)
                    sp.dma_start(ctx_dram[b, g * HG:(g + 1) * HG].rearrange("h r n -> (h r) n"),
                                 pv_sb[:, g % 2, :]).then_inc(pv_stored[g], DMA)

                def load_ctx(b):
                    for g in range(NG):
                        wait_apart(sp, pv_stored[g], (b + 1) * DMA)
                    sp.dma_start(sums[:, :], ctx_dram[b, :, D, :].rearrange("h (a n) -> h a n", a=P // H)
                                 ).then_inc(sums_loaded, DMA)
                    if not (isinstance(b, int) and b == 0):
                        wait_apart(sp, wo_made, b * CT)
                    for t in range(CT):
                        sp.dma_start(ctx_raw[:, t, :], ctx_dram[b].rearrange("(h t) r n -> t h r n", t=CT)[t, :, 0:D, :]
                                     ).then_inc(ctx_loaded, DMA)

                def spread_inverse(b):
                    wait_apart(sp, inverted, b + 1)
                    sp.dma_start(inv_dram[b].rearrange("h (a n) -> h a n", a=P // H), sums[:, :]
                                 ).then_inc(inv_stored, DMA)
                    wait_apart(sp, inv_stored, (b + 1) * DMA)
                    for t in range(CT):
                        sp.dma_start(inv_sum[:, t, :], inv_dram[b].rearrange("(h t) n -> t h n", t=CT)[t]
                                     .unsqueeze(1).to_broadcast([HPT, D, T])).then_inc(inv_loaded, DMA)

                def store_r(b):
                    wait_apart(sp, r_done, b * CT + CT)
                    sp.dma_start(r_dram[b].rearrange("(t p) n -> p t n", p=P), r_out[:, :, :]
                                 ).then_inc(r_stored, DMA)

                def save_q(b):
                    wait_apart(sp, ln_done["q"], b * 2 + 2)
                    if not (isinstance(b, int) and b == 0):
                        wait_apart(sp, q_kept, b * DMA)
                    sp.dma_start(q_mid[:, :, :], ln["q"][:, :, :]).then_inc(q_saved, DMA)

                def keep_q(b):
                    wait_apart(sp, q_saved, b * DMA + DMA)
                    if not (isinstance(b, int) and b == 0):
                        wait_apart(sp, r_done, b * CT)
                    sp.dma_start(q_res[:, :, :], q_mid[:, :, :]).then_inc(q_kept, DMA)

                def batch(b, first=False, last=False, load_more=True):
                    fill_stack(b, NG - 1)
                    if not first:
                        store_pv(b - 1, NG - 1)
                        load_ctx(b - 1)
                    if load_more:
                        load(b + 2, "k")
                        load(b + 2, "q")
                    if not first:
                        spread_inverse(b - 1)
                    store_pv(b, 0)
                    if not first:
                        store_r(b - 1)
                    keep_q(b)
                    if not last:
                        fill_stack(b + 1, 0)
                        fill_stack(b + 1, 1)
                        save_q(b + 1)
                    store_pv(b, 1)
                    if not last:
                        fill_stack(b + 1, 2)
                    store_pv(b, 2)

                load(0, "k")
                sp.dma_start(pe_tab[:, :, :], pos.rearrange("(t p) n -> p t n", p=P)).then_inc(weights, DMA)
                load(0, "q")
                load(1, "k")
                load(1, "q")
                for g in range(NG - 1):
                    fill_stack(0, g)
                save_q(0)
                batch(0, first=True)
                with sp.Fori(1, B - 2) as b:
                    batch(b)
                batch(B - 2, load_more=False)
                batch(B - 1, last=True, load_more=False)
                store_pv(B - 1, NG - 1)
                load_ctx(B - 1)
                spread_inverse(B - 1)
                store_r(B - 1)
                sp.wait_ge(r_stored, B * DMA)

            @block.gpsimd
            def _(pool):
                def add_pos(b, n):
                    pool.wait_ge(loaded[n], b * DMA + DMA)
                    pool.tensor_tensor(src[n][:, :, :], src[n][:, :, :], pe_tab[:, :, :], ALU.add
                                       ).then_inc(pos_added[n], 1)

                def inv_std(b, n):
                    wait_apart(pool, stat_done[n], b * KC + KC)
                    pool.tensor_scalar(rstd[n][:, :], mv[n][:, :, 1], EPS, None, ALU.add
                                       ).then_inc(rstd_step[n], 1)
                    pool.wait_ge(rstd_step[n], b * 2 + 1)
                    pool.tensor_tensor(rstd[n][:, :], rstd[n][:, :], neg_half[:, :], ALU.pow
                                       ).then_inc(rstd_step[n], 1)

                def normalise(b, n):
                    wait_apart(pool, rstd_step[n], b * 2 + 2)
                    for c in range(KC):
                        pool.tensor_scalar(tok[n][:, c, :], tok[n][:, c, :], mv[n][:, c, 0:1],
                                           rstd[n][:, c:c + 1], ALU.subtract, ALU.mult
                                           ).then_inc(normed[n], 1)

                def batch(b, last=False, load_more=True):
                    if not last:
                        inv_std(b + 1, "k")
                        inv_std(b + 1, "q")
                        normalise(b + 1, "k")
                    if load_more:
                        add_pos(b + 2, "k")
                        add_pos(b + 2, "q")

                pool.memset(ident[:, :], 0.0).then_inc(consts, 1)
                pool.memset(neg_half[:, :], -0.5).then_inc(consts, 1)
                pool.wait_ge(consts, 2)
                pool.affine_select(out=ident[:, :], in_=ident[:, :], compare_op=ALU.not_equal, fill=1.0,
                                   base=0, pattern=[[-1, P]], channel_multiplier=1).then_inc(consts, 1)
                pool.wait_ge(consts, 3)
                pool.memset(stacks[ZROW:P, :, :].bitcast(F32), 0.0).then_inc(consts, 1)
                pool.wait_ge(consts, 4)
                pool.memset(stacks[ONES:P, :, 0].bitcast(F32), 1.0).then_inc(consts, 1)
                pool.wait_ge(consts, 5)
                pool.memset(lo_rows[:, :], -1.0).then_inc(consts, 1)
                pool.wait_ge(consts, 6)
                pool.memset(lo_rows[0:HG * KC, :], 0.0).then_inc(consts, 1)
                pool.wait_ge(consts, 7)
                pool.wait_ge(weights, 12 * DMA)
                add_pos(0, "k")
                add_pos(0, "q")
                pool.memset(v_ones[:, :, :, D:2 * D], 1.0).then_inc(consts, 1)
                inv_std(0, "k")
                inv_std(0, "q")
                normalise(0, "k")
                add_pos(1, "k")
                add_pos(1, "q")
                batch(0)
                with pool.Fori(1, B - 2) as b:
                    batch(b)
                batch(B - 2, load_more=False)
                batch(B - 1, last=True, load_more=False)

            @block.scalar
            def _(act):
                def take_tok(b, n, half):
                    act.wait_ge(tr_in[n], b * 2 + half + 1)
                    if half == 0 and not (isinstance(b, int) and b == 0):
                        act.wait_ge(tr_out[n], b * 2)
                    act.activation(tok[n][:, 2 * half:2 * half + 2, :], tr_ps[:, :], ACT.Copy
                                   ).then_inc(tok_ready[n], 1)

                def take_ln(b, n, t):
                    act.wait_ge(tr_out[n], b * 2 + t + 1)
                    if t == 0 and not (isinstance(b, int) and b == 0):
                        act.wait_ge(proj[n], b * 2)
                        if n == "k":
                            act.wait_ge(v_made, b * KC)
                        else:
                            act.wait_ge(q_saved, b * DMA)
                    act.activation(ln[n][:, t, :], tr_ps[:, :], ACT.Identity,
                                   scale=gain[n][:, t:t + 1], bias=bias[n][:, t:t + 1]
                                   ).then_inc(ln_done[n], 1)

                def take_hi(b, n, t):
                    act.wait_ge(proj[n], b * 2 + t + 1)
                    if not (isinstance(b, int) and b == 0):
                        if n == "k" and t == 0:
                            for g in range(NG):
                                act.wait_ge(stacked[g], b * STACK)
                    act.activation(hi[n][:, t, :], qk_ps[n][:, :], ACT.Copy).then_inc(hi_done[n], 1)

                def take_v(b, c):
                    act.wait_ge(v_made, b * KC + c + 1)
                    if not (isinstance(b, int) and b == 0):
                        act.wait_ge(pv_made, b * STEPS + c + 1 - KC)
                    act.activation(v_ones[:, c, :, 0:D],
                                   xc_ps[:, 0:C].rearrange("p (h d) -> p h d", d=D), ACT.Copy
                                   ).then_inc(v_done, 1)

                def exp(b, s, j, first=False):
                    act.wait_ge(sc_made, unit_of(b, s, j) + 1)
                    if j == 0 and not (first and s < 2):
                        act.wait_ge(pv_made, b * STEPS + s - 1)
                    act.activation(probs[:, s % 2, j, :], sc_ps[j % 2][:, :], ACT.Exp, scale=SCALE
                                   ).then_inc(exp_done, 1)

                def place_max(b, g):
                    act.wait_ge(mlo_done, b * NG + g + 1)
                    act.dma_start(stacks[MROW:MROW + 2, g, 1, :, :, :].bitcast(F32),
                                 m_both[:, :].bitcast(F32)).then_inc(m_placed[g], DMA)

                def take_pv(b, g, first=False):
                    act.wait_ge(pv_made, b * STEPS + (g + 1) * KC)
                    if g >= 2:
                        act.wait_ge(pv_stored[g - 2], (b + 1) * DMA)
                    elif not first:
                        act.wait_ge(pv_stored[g + 2], b * DMA)
                    act.activation(pv_sb[:, g % 2, :], pv_ps[:, :], ACT.Copy).then_inc(pv_out, 1)

                def batch(b, first=False, last=False):
                    for s in range(STEPS):
                        exp(b, s, 0, first)
                        if s == 1:
                            take_v(b, 3)
                        if s == 1 and not last:
                            take_tok(b + 1, "k", 1)
                        if s == 2 and not last:
                            take_tok(b + 1, "q", 1)
                        if s == 5 and not last:
                            take_ln(b + 1, "k", 1)
                        if s == 6 and not last:
                            take_ln(b + 1, "q", 1)
                            take_hi(b + 1, "k", 0)
                        if s == 7 and not last:
                            take_hi(b + 1, "k", 1)
                        if s == 14 and not last:
                            take_v(b + 1, 0)
                        if s == 15 and not last:
                            take_v(b + 1, 1)
                        if s == 0 and not first:
                            take_v(b, 2)
                        exp(b, s, 1, first)
                        if s % KC == KC - 1 and s + 1 < STEPS:
                            place_max(b, (s + 1) // KC)
                        elif s % KC == KC - 1 and not last:
                            place_max(b + 1, 0)
                        exp(b, s, 2, first)
                        if s % KC == 0 and s:
                            take_pv(b, s // KC - 1, first)
                        if s == 0 and not first:
                            take_pv(b - 1, NG - 1)
                        if s == 0 and not last:
                            take_tok(b + 1, "k", 0)
                        if s == 1 and not last:
                            take_tok(b + 1, "q", 0)
                        if s == 4 and not last:
                            take_ln(b + 1, "k", 0)
                        if s == 5 and not last:
                            take_ln(b + 1, "q", 0)
                        if s in (6, 7) and not last:
                            take_hi(b + 1, "q", s - 6)
                        exp(b, s, 3, first)

                act.dma_start(w_k[:, :, :], Wk.rearrange("(t p) n -> p t n", p=P)).then_inc(weights, DMA)
                act.dma_start(w_q[:, :, :], Wq.rearrange("(t p) n -> p t n", p=P)).then_inc(weights, DMA)
                act.dma_start(w_v[:, :, :], Wv.rearrange("(t p) n -> p t n", p=P)).then_inc(weights, DMA)
                act.dma_start(w_o[:, :, :], Wo.rearrange("(t p) n -> p t n", p=P)).then_inc(weights, DMA)
                for dst, v in ((gq, ln_q_g), (bq, ln_q_b), (gk, ln_kv_g), (bk, ln_kv_b),
                               (gf, ffn_g), (bf, ffn_b), (b2_col, b2)):
                    act.dma_start(dst, v.rearrange("(t p) -> p t", p=P),
                                  allow_slow_non_contiguous=True).then_inc(weights, DMA)
                act.wait_ge(weights, 12 * DMA)
                for n in "kq":
                    for half in range(2):
                        take_tok(0, n, half)
                for n in "kq":
                    for t in range(CT):
                        take_ln(0, n, t)
                for n in "kq":
                    for t in range(CT):
                        take_hi(0, n, t)
                for c in range(3):
                    take_v(0, c)
                place_max(0, 0)
                batch(0, first=True)
                with act.Fori(1, B - 1) as b:
                    batch(b)
                batch(B - 1, last=True)
                take_pv(B - 1, NG - 1)

            @block.vector
            def _(dve):
                def stats(b, n):
                    for c in range(KC):
                        dve.wait_ge(tok_ready[n], b * 2 + c // 2 + 1)
                        dve.bn_stats(stat[n][:, c, :], tok[n][:, c, :]).then_inc(bn_done[n], 1)
                    if not (isinstance(b, int) and b == 0):
                        wait_apart(dve, normed[n], b * KC)
                    for c in range(KC):
                        wait_apart(dve, bn_done[n], b * KC + c + 1)
                        dve.bn_aggr(mv[n][:, c, :], stat[n][:, c, :]).then_inc(stat_done[n], 1)

                def normalise_q(b):
                    dve.wait_ge(rstd_step["q"], b * 2 + 2)
                    for c in range(KC):
                        dve.tensor_scalar(tok["q"][:, c, :], tok["q"][:, c, :], mv["q"][:, c, 0:1],
                                          rstd["q"][:, c:c + 1], ALU.subtract, ALU.mult
                                          ).then_inc(normed["q"], 1)

                def take_lo(b, n, t):
                    dve.wait_ge(hi_done[n], b * 2 + t + 1)
                    dve.tensor_tensor(lo[n][:, t, :], qk_ps[n][:, :], hi[n][:, t, :].bitcast(F32),
                                      ALU.subtract).then_inc(lo_done[n], 1)

                def row_max(b, q, j, first=False):
                    g, c = q // KC, q % KC
                    dve.wait_ge(mx_made, unit_of(b, q, j) + 1)
                    if c == 0 and j == 0 and not (first and g < 2):
                        dve.wait_ge(mt_made, b * NG + g - 1)
                    dve.tensor_reduce(neg_max[:, g % 2, 0, j * KC + c:j * KC + c + 1], mx_ps[j % 2][:, :],
                                      AX_X, ALU.max, negate=True).then_inc(mx_done, 1)

                def repeat_max(b, g):
                    dve.wait_ge(mx_done, unit_of(b, (g + 1) * KC, 0))
                    dve.tensor_copy(neg_max[:, g % 2, 1, :], neg_max[:, g % 2, 0, :]).then_inc(mx_twice, 1)

                def split_max(b, g, first=False):
                    dve.wait_ge(mt_made, b * NG + g + 1)
                    dve.tensor_copy(m_hi[:, :], xc_ps[0:2 * HG * KC, 0:P]).then_inc(mhi_done, 1)
                    if g >= 1:
                        dve.wait_ge(m_placed[g - 1], b * DMA + DMA)
                    elif not first:
                        dve.wait_ge(m_placed[NG - 1], b * DMA)
                    dve.wait_ge(mhi_done, b * NG + g + 1)
                    dve.scalar_tensor_tensor(m_both[:, :], m_hi[:, :].bitcast(F32), lo_rows[:, 0:1],
                                             xc_ps[0:2 * HG * KC, 0:P], ALU.mult, ALU.add
                                             ).then_inc(mlo_done, 1)

                def invert_sums(b):
                    dve.wait_ge(sums_loaded, b * DMA + DMA)
                    dve.reciprocal(sums[:, :], sums[:, :]).then_inc(inverted, 1)

                def scale_ctx(b):
                    dve.wait_ge(ctx_loaded, (b + 1) * 2 * DMA)
                    dve.wait_ge(inv_loaded, (b + 1) * 2 * DMA)
                    for t in range(CT):
                        dve.tensor_tensor(ctx_raw[:, t, :], ctx_raw[:, t, :], inv_sum[:, t, :], ALU.mult
                                          ).then_inc(ctx_done, 1)

                def add_q(b, t):
                    dve.wait_ge(wo_made, b * CT + t + 1)
                    if t == 0:
                        dve.wait_ge(q_kept, b * DMA + DMA)
                        if not (isinstance(b, int) and b == 0):
                            dve.wait_ge(r_stored, b * DMA)
                    dve.tensor_tensor(r_out[:, t, :], xc_ps[:, :], q_res[:, t, :], ALU.add
                                      ).then_inc(r_done, 1)

                def batch(b, first=False, last=False):
                    for s in range(STEPS):
                        q = s + LEAD
                        nb, nq = (b, q) if q < STEPS else (b + 1, q - STEPS)
                        todo = q < STEPS or not last
                        if todo:
                            row_max(nb, nq, 0, first and q < STEPS)
                        if s == 1 and not last:
                            stats(b + 1, "k")
                        if s == 2 and not last:
                            stats(b + 1, "q")
                        if s == 2 and not first:
                            invert_sums(b - 1)
                        if s == 3 and not last:
                            normalise_q(b + 1)
                        if s == 4 and not first:
                            scale_ctx(b - 1)
                        if s == 5 and not first:
                            add_q(b - 1, 0)
                        if s == 6 and not last:
                            take_lo(b + 1, "k", 0)
                        if s == 7 and not last:
                            take_lo(b + 1, "k", 1)
                        if todo:
                            row_max(nb, nq, 1, first and q < STEPS)
                            row_max(nb, nq, 2, first and q < STEPS)
                        if s % KC == 2 and s + 2 < STEPS:
                            split_max(b, (s + 2) // KC)
                        if s + 2 == STEPS and not last:
                            split_max(b + 1, 0)
                        if s == 5 and not first:
                            add_q(b - 1, 1)
                        if s in (6, 7) and not last:
                            take_lo(b + 1, "q", s - 6)
                        if todo:
                            row_max(nb, nq, 3, first and q < STEPS)
                        if q % KC == KC - 1 and todo:
                            repeat_max(nb, nq // KC)

                stats(0, "k")
                stats(0, "q")
                normalise_q(0)
                for n in "kq":
                    for t in range(CT):
                        take_lo(0, n, t)
                for q in range(LEAD):
                    for j in range(HG):
                        row_max(0, q, j, True)
                    if q == KC - 1:
                        repeat_max(0, 0)
                        split_max(0, 0, True)
                batch(0, first=True)
                with dve.Fori(1, B - 1) as b:
                    batch(b)
                batch(B - 1, last=True)
                invert_sums(B - 1)
                scale_ctx(B - 1)
                for t in range(CT):
                    add_q(B - 1, t)

            @block.tensor
            def _(pe):
                def transpose_in(b, n, half):
                    if half == 0:
                        pe.wait_ge(pos_added[n], b + 1)
                    if half == 1:
                        pe.wait_ge(tok_ready[n], b * 2 + 1)
                    elif n == "q":
                        pe.wait_ge(tok_ready["k"], b * 2 + 2)
                    elif not (isinstance(b, int) and b == 0):
                        pe.wait_ge(lo_done["q"], b * 2)
                    for c in range(2):
                        for t in range(CT):
                            at = c * C + t * P
                            m = pe.transpose(tr_ps[:, at:at + P],
                                             src[n][:, t, (2 * half + c) * P:(2 * half + c + 1) * P],
                                             ident[:, :])
                    m.then_inc(tr_in[n], 1)

                def transpose_out(b, n, t):
                    if t == 0:
                        pe.wait_ge(normed[n], b * KC + KC)
                    if t == 1:
                        pe.wait_ge(ln_done[n], b * 2 + 1)
                    elif n == "k":
                        pe.wait_ge(tok_ready["q"], b * 2 + 2)
                    else:
                        pe.wait_ge(ln_done["k"], b * 2 + 2)
                    for c in range(KC):
                        m = pe.transpose(tr_ps[:, c * P:(c + 1) * P], tok[n][:, c, t * P:(t + 1) * P],
                                         ident[:, :])
                    m.then_inc(tr_out[n], 1)

                def project(b, n, t):
                    if t == 0:
                        pe.wait_ge(ln_done[n], b * 2 + 2)
                    if t == 1:
                        pe.wait_ge(lo_done[n], b * 2 + 1)
                    elif n == "k" and not (isinstance(b, int) and b == 0):
                        pe.wait_ge(lo_done["k"], b * 2)
                    for k in range(CT):
                        m = pe.matmul(qk_ps[n][:, :], w_of[n][:, k, t * P:(t + 1) * P], ln[n][:, k, :],
                                      start=(k == 0), stop=(k == CT - 1))
                    m.then_inc(proj[n], 1)

                def make_v(b, c):
                    if c == 0:
                        pe.wait_ge(ln_done["k"], b * 2 + 2)
                        if not (isinstance(b, int) and b == 0):
                            pe.wait_ge(mlo_done, b * NG)
                    elif c == 1 and not (isinstance(b, int) and b == 0):
                        pe.wait_ge(mlo_done, b * NG + 1)
                    elif c == 3 and isinstance(b, int) and b == 0:
                        pe.wait_ge(mlo_done, 1)
                    else:
                        pe.wait_ge(v_done, b * KC + c)
                    for k in range(CT):
                        m = pe.matmul(xc_ps[:, 0:C], ln["k"][:, k, c * P:(c + 1) * P], w_v[:, k, :],
                                      start=(k == 0), stop=(k == CT - 1))
                    m.then_inc(v_made, 1)

                def transpose_max(b, g, first=False, last=False):
                    pe.wait_ge(mx_twice, b * NG + g + 1)
                    if g == 0:
                        pe.wait_ge(v_done, b * KC + (3 if first else 1))
                    elif g == 1:
                        pe.wait_ge(v_done, b * KC + KC)
                    elif g == 2 and not first:
                        pe.wait_ge(r_done, b * CT)
                    else:
                        pe.wait_ge(mlo_done, b * NG + g)
                    pe.transpose(xc_ps[0:2 * HG * KC, 0:P], neg_max[:, g % 2, :, :], ident[:, :]
                                 ).then_inc(mt_made, 1)

                def max_scores(b, q, j, fresh=False):
                    g, c = q // KC, q % KC
                    if c == 0 and j == 0:
                        pe.wait_ge(stacked[g], b * STACK + STACK)
                    if not (fresh and q == 0 and j < 2):
                        pe.wait_ge(mx_done, unit_of(b, q, j) - 1)
                    k_rows, q_rows = (stacks[0:MROW, g, n, j // CT, j % CT, :] for n in (0, 1))
                    pe.matmul(mx_ps[j % 2][:, :], q_rows[:, c * P:(c + 1) * P], k_rows,
                              start=True, stop=True).then_inc(mx_made, 1)

                def scores(b, s, j, first=False):
                    g, c = s // KC, s % KC
                    if c == 0 and j == 0:
                        pe.wait_ge(m_placed[g], b * DMA + DMA)
                    if not (first and s == 0 and j < 2):
                        pe.wait_ge(exp_done, unit_of(b, s, j) - 1)
                    k_rows, q_rows = (stacks[:, g, n, j // CT, j % CT, :] for n in (0, 1))
                    pe.matmul(sc_ps[j % 2][:, :], k_rows[:, c * P:(c + 1) * P], q_rows,
                              start=True, stop=True).then_inc(sc_made, 1)

                def prob_value(b, s, first=False):
                    g, c = s // KC, s % KC
                    pe.wait_ge(exp_done, unit_of(b, s + 1, 0))
                    pe.wait_ge(v_done, b * KC + c + 1)
                    if c == 0 and not (first and g == 0):
                        pe.wait_ge(pv_out, b * NG + g)
                    for j in range(HG):
                        m = pe.matmul(pv_ps[32 * j:32 * j + 32, :], v_ones[:, c, head(g, j), :],
                                      probs[:, s % 2, j, :], start=(c == 0), stop=(c == KC - 1))
                    m.then_inc(pv_made, 1)

                def out_proj(b, t, b_next=True):
                    if t == 0:
                        pe.wait_ge(ctx_done, b * CT + CT)
                        pe.wait_ge(mlo_done, b * NG + NG + (2 if b_next else 0))
                    else:
                        pe.wait_ge(r_done, b * CT + 1)
                    for k in range(CT):
                        m = pe.matmul(xc_ps[:, :], w_o[:, k, t * P:(t + 1) * P], ctx_raw[:, k, :],
                                      start=(k == 0), stop=(k == CT - 1))
                    m.then_inc(wo_made, 1)

                def batch(b, first=False, last=False):
                    for s in range(STEPS):
                        q = s + LEAD
                        nb, nq = (b, q) if q < STEPS else (b + 1, q - STEPS)
                        todo = q < STEPS or not last
                        for j in (0, 1):
                            scores(b, s, j, first)
                            if todo:
                                max_scores(nb, nq, j)
                        if s % KC == 2:
                            if s + 2 < STEPS:
                                transpose_max(b, (s + 2) // KC, first)
                            elif not last:
                                transpose_max(b + 1, 0)
                        if s:
                            prob_value(b, s - 1, first)
                        elif not first:
                            prob_value(b - 1, STEPS - 1)
                        if s == 5 and not first:
                            out_proj(b - 1, 1)
                        if not last:
                            if s == 0:
                                transpose_in(b + 1, "k", 0)
                            if s == 1:
                                transpose_in(b + 1, "q", 0)
                            if s == 4:
                                transpose_out(b + 1, "k", 0)
                            if s == 5:
                                transpose_out(b + 1, "q", 0)
                            if s in (6, 7):
                                project(b + 1, "q", s - 6)
                        for j in (2, 3):
                            scores(b, s, j, first)
                            if todo:
                                max_scores(nb, nq, j)
                        if s == 0:
                            make_v(b, 3)
                        if s == 4 and not first:
                            out_proj(b - 1, 0)
                        if last:
                            continue
                        if s == 0:
                            transpose_in(b + 1, "k", 1)
                        if s == 1:
                            transpose_in(b + 1, "q", 1)
                        if s == 4:
                            transpose_out(b + 1, "k", 1)
                        if s == 5:
                            transpose_out(b + 1, "q", 1)
                        if s in (5, 6):
                            project(b + 1, "k", s - 5)
                        if s in (13, 14, 15):
                            make_v(b + 1, s - 13)

                pe.wait_ge(consts, 8)
                pe.wait_ge(weights, 12 * DMA)
                for n in "kq":
                    for half in range(2):
                        transpose_in(0, n, half)
                for n in "kq":
                    for t in range(CT):
                        transpose_out(0, n, t)
                for n in "kq":
                    for t in range(CT):
                        project(0, n, t)
                for c in range(3):
                    make_v(0, c)
                for q in range(LEAD):
                    for j in range(HG):
                        max_scores(0, q, j, fresh=True)
                    if q == KC - 1:
                        transpose_max(0, 0, first=True)
                batch(0, first=True)
                with pe.Fori(1, B - 1) as b:
                    batch(b)
                batch(B - 1, last=True)
                prob_value(B - 1, STEPS - 1)
                for t in range(CT):
                    out_proj(B - 1, t, b_next=False)

        r_buf = sb("r_buf", [P, 2, CT, T])
        h_buf = sb("h_buf", [P, 2, CT, T])
        act_buf = sb("act_buf", [P, FT, T])
        tok_f = tok["k"]
        out_buf = x_in
        stat_f, mv_f, rstd_f = stat["k"], mv["k"], rstd["k"]
        up_ps, down_ps = sc_ps + mx_ps, [pv_ps, pj_ps]
        t_ps = [tr_ps, xc_ps]

        ffw_weights = sem("ffw_weights")
        r_loaded = [sem("r_loaded0"), sem("r_loaded1")]
        f_tr_in = sem("f_tr_in")
        f_tok = sem("f_tok")
        f_bn = sem("f_bn")
        f_stat = sem("f_stat")
        f_rstd = sem("f_rstd")
        f_normed = sem("f_normed")
        f_tr_out = sem("f_tr_out")
        f_ln = sem("f_ln")
        up_made = sem("up_made")
        gelu_done = sem("gelu_done")
        down_made = sem("down_made")
        out_done = sem("out_done")
        out_stored = sem("out_stored")

        with nc.Block() as block:
            def zero(b):
                return isinstance(b, int) and b == 0

            def pairs(eng, batch):
                batch(0, 0)
                batch(1, 1)
                with eng.Fori(1, B // 2 - 1) as i:
                    batch(2 * i, 0)
                    batch(2 * i + 1, 1)
                batch(B - 2, 0)
                batch(B - 1, 1, last=True)

            @block.sync
            def _(sp):
                def load_r(b, i):
                    if not (isinstance(b, int) and b < 2):
                        wait_apart(sp, out_done, b * CT - CT)
                    sp.dma_start(r_buf[:, i, :, :], r_dram[b].rearrange("(t p) n -> p t n", p=P)
                                 ).then_inc(r_loaded[i], DMA)

                def store(b):
                    wait_apart(sp, out_done, b * CT + CT)
                    sp.dma_start(out[b].rearrange("(t p) n -> p t n", p=P), out_buf[:, :, :]
                                 ).then_inc(out_stored, DMA)

                load_r(0, 0)
                sp.dma_start(w_1[:, :, :], W1.rearrange("(t p) n -> p t n", p=P)).then_inc(ffw_weights, DMA)
                sp.dma_start(w_2[:, :, :], W2.rearrange("(t p) n -> p t n", p=P)).then_inc(ffw_weights, DMA)
                sp.dma_start(b1_col[:, :], b1.rearrange("(t p) -> p t", p=P),
                             allow_slow_non_contiguous=True).then_inc(ffw_weights, DMA)
                load_r(1, 1)
                with sp.Fori(0, B // 2 - 1) as i:
                    load_r(2 * i + 2, 0)
                    store(2 * i)
                    load_r(2 * i + 3, 1)
                    store(2 * i + 1)
                store(B - 2)
                store(B - 1)
                sp.wait_ge(out_stored, B * DMA)

            @block.gpsimd
            def _(pool):
                def inv_std(b):
                    wait_apart(pool, f_stat, b * KC + KC)
                    if not zero(b):
                        pool.wait_ge(f_normed, b * KC)
                    pool.tensor_scalar(rstd_f[:, :], mv_f[:, :, 1], EPS, None, ALU.add).then_inc(f_rstd, 1)
                    pool.wait_ge(f_rstd, b * 2 + 1)
                    pool.tensor_tensor(rstd_f[:, :], rstd_f[:, :], neg_half[:, :], ALU.pow
                                       ).then_inc(f_rstd, 1)

                inv_std(0)
                with pool.Fori(1, B) as b:
                    inv_std(b)

            @block.scalar
            def _(act):
                def take_tok(b, half):
                    act.wait_ge(f_tr_in, b * 2 + half + 1)
                    if half == 0 and not zero(b):
                        act.wait_ge(f_tr_out, b * 2)
                    act.activation(tok_f[:, 2 * half:2 * half + 2, :], t_ps[half][:, :], ACT.Copy
                                   ).then_inc(f_tok, 1)

                def take_ln(b, i, t):
                    act.wait_ge(f_tr_out, b * 2 + t + 1)
                    if not (isinstance(b, int) and b < 2):
                        act.wait_ge(up_made, b * FT - FT)
                    act.activation(h_buf[:, i, t, :], t_ps[t][:, :], ACT.Identity,
                                   scale=gf[:, t:t + 1], bias=bf[:, t:t + 1]).then_inc(f_ln, 1)

                def gelu(b, f):
                    act.wait_ge(up_made, b * FT + f + 1)
                    if f == 0 and not zero(b):
                        act.wait_ge(down_made, b * CT)
                    act.activation(act_buf[:, f, :], up_ps[f][:, :], ACT.Gelu,
                                   bias=b1_col[:, f:f + 1]).then_inc(gelu_done, 1)

                def batch(b, i, last=False):
                    for f in range(FT):
                        gelu(b, f)
                        if f == 1 and not last:
                            take_tok(b + 1, 0)
                            take_tok(b + 1, 1)
                    if not last:
                        take_ln(b + 1, 1 - i, 0)
                        take_ln(b + 1, 1 - i, 1)

                act.wait_ge(ffw_weights, 3 * DMA)
                take_tok(0, 0)
                take_tok(0, 1)
                take_ln(0, 0, 0)
                take_ln(0, 0, 1)
                pairs(act, batch)

            @block.vector
            def _(dve):
                def normalise(b):
                    for c in range(KC):
                        dve.wait_ge(f_tok, b * 2 + c // 2 + 1)
                        dve.bn_stats(stat_f[:, c, :], tok_f[:, c, :]).then_inc(f_bn, 1)
                    for c in range(KC):
                        wait_apart(dve, f_bn, b * KC + c + 1)
                        dve.bn_aggr(mv_f[:, c, :], stat_f[:, c, :]).then_inc(f_stat, 1)
                    dve.wait_ge(f_rstd, b * 2 + 2)
                    for c in range(KC):
                        dve.tensor_scalar(tok_f[:, c, :], tok_f[:, c, :], mv_f[:, c, 0:1],
                                          rstd_f[:, c:c + 1], ALU.subtract, ALU.mult
                                          ).then_inc(f_normed, 1)

                def finish(b, i, t):
                    dve.wait_ge(down_made, b * CT + t + 1)
                    if t == 0 and not zero(b):
                        dve.wait_ge(out_stored, b * DMA)
                    if t == 0:
                        dve.wait_ge(ffw_weights, 3 * DMA)
                    dve.scalar_tensor_tensor(out_buf[:, t, :], down_ps[t][:, :], b2_col[:, t:t + 1],
                                             r_buf[:, i, t, :], ALU.add, ALU.add).then_inc(out_done, 1)

                def batch(b, i, last=False):
                    if not last:
                        normalise(b + 1)
                    finish(b, i, 0)
                    finish(b, i, 1)

                normalise(0)
                pairs(dve, batch)

            @block.tensor
            def _(pe):
                def transpose_in(b, i, half):
                    if half == 0:
                        pe.wait_ge(r_loaded[i], (b - i) * (DMA // 2) + DMA)
                        if not zero(b):
                            pe.wait_ge(f_ln, b * 2)
                    for c in range(2):
                        for t in range(CT):
                            at = c * C + t * P
                            m = pe.transpose(t_ps[half][:, at:at + P],
                                             r_buf[:, i, t, (2 * half + c) * P:(2 * half + c + 1) * P],
                                             ident[:, :])
                    m.then_inc(f_tr_in, 1)

                def transpose_out(b, t):
                    if t == 0:
                        pe.wait_ge(f_normed, b * KC + KC)
                        pe.wait_ge(f_tok, b * 2 + 2)
                    for c in range(KC):
                        m = pe.transpose(t_ps[t][:, c * P:(c + 1) * P], tok_f[:, c, t * P:(t + 1) * P],
                                         ident[:, :])
                    m.then_inc(f_tr_out, 1)

                def up(b, i, f):
                    if f == 0:
                        pe.wait_ge(f_ln, b * 2 + 2)
                    if not zero(b):
                        pe.wait_ge(gelu_done, b * FT - FT + f + 1)
                    for k in range(CT):
                        m = pe.matmul(up_ps[f][:, :], w_1[:, k, f * P:(f + 1) * P], h_buf[:, i, k, :],
                                      start=(k == 0), stop=(k == CT - 1))
                    m.then_inc(up_made, 1)

                def down(b, t):
                    if not zero(b):
                        pe.wait_ge(out_done, b * CT - CT + t + 1)
                    for f in range(FT):
                        if t == 0:
                            pe.wait_ge(gelu_done, b * FT + f + 1)
                        m = pe.matmul(down_ps[t][:, :], w_2[:, f, t * P:(t + 1) * P], act_buf[:, f, :],
                                      start=(f == 0), stop=(f == FT - 1))
                    m.then_inc(down_made, 1)

                def batch(b, i, last=False):
                    for f in range(FT):
                        up(b, i, f)
                        if f == 1 and not last:
                            transpose_in(b + 1, 1 - i, 0)
                            transpose_in(b + 1, 1 - i, 1)
                    down(b, 0)
                    if not last:
                        transpose_out(b + 1, 0)
                        transpose_out(b + 1, 1)
                    down(b, 1)

                pe.wait_ge(ffw_weights, 3 * DMA)
                transpose_in(0, 0, 0)
                transpose_in(0, 0, 1)
                transpose_out(0, 0)
                transpose_out(0, 1)
                pairs(pe, batch)


_INS = ['x', 'ctx_2048', 'L0_xattn_Wq', 'L0_xattn_Wk', 'L0_xattn_Wv', 'L0_xattn_Wo', 'L0_xattn_ln_q_g',
        'L0_xattn_ln_q_b', 'L0_xattn_ln_kv_g', 'L0_xattn_ln_kv_b', 'L0_xattn_ffn_ln_g', 'L0_xattn_ffn_ln_b',
        'L0_xattn_W1', 'L0_xattn_b1', 'L0_xattn_W2', 'L0_xattn_b2']
_OUTS = [((16, 256, 512), 'float32')]


def positions(c, t):
    import math
    import numpy as np
    f = np.float32
    div = np.exp((np.arange(0, c, 2, dtype=f) * f(-math.log(10000.0) / c)).astype(np.float64)).astype(f)
    ang = (np.arange(t, dtype=f)[:, None] * div).astype(np.float64)
    pe = np.zeros((t, c), f)
    pe[:, 0::2] = np.sin(ang)
    pe[:, 1::2] = np.cos(ang)
    return np.ascontiguousarray(pe.T)


def kernel(**inputs):
    import numpy as _np
    import concourse.bacc as _bacc
    from concourse import mybir as _mybir
    from concourse.bass_utils import run_bass_kernel_spmd as _run

    nc = _bacc.Bacc("TRN2", target_bir_lowering=False, num_devices=1)
    arrays, args = {}, []
    for name in _INS:
        a = _np.ascontiguousarray(inputs[name])
        arrays[f"in_{name}_dram"] = a
        args.append(nc.dram_tensor(f"in_{name}_dram", a.shape, _mybir.dt.from_np(a.dtype), kind="ExternalInput").ap())
    table = positions(inputs["x"].shape[1], inputs["x"].shape[2])
    arrays["in_positions_dram"] = table
    args.append(nc.dram_tensor("in_positions_dram", table.shape, _mybir.dt.from_np(table.dtype), kind="ExternalInput").ap())
    for i, (shape, dtype) in enumerate(_OUTS):
        dt = _mybir.dt.from_np(_np.dtype(dtype))
        args.append(nc.dram_tensor(f"out_{i}_dram", shape, dt, kind="ExternalOutput").ap())
    xattn_kernel(nc, *args)
    r = _run(nc, [arrays], core_ids=[0])
    return r.results[0]["out_0_dram"]
```

```python
from contextlib import ExitStack

import concourse.bass as bass
from concourse import mybir

F32 = mybir.dt.float32
F32R = mybir.dt.float32r
ALU = mybir.AluOpType
ACT = mybir.ActivationFunctionType
AX_X = mybir.AxisListType.X

P = 128
D = 16
HG = 4
EPS = 1e-5
TERMS = 4
REST = TERMS * D
MROW = P - 2
DMA = 16


def xattn_kernel(nc, x, ctx_in, Wq, Wk, Wv, Wo, ln_q_g, ln_q_b, ln_kv_g, ln_kv_b,
                 ffn_g, ffn_b, W1, b1, W2, b2, pos, out):
    B, C, T = x.shape
    H = C // D
    CT = C // P
    KC = T // P
    NG = H // HG
    STEPS = NG * KC
    UNITS = STEPS * HG
    F = W1.shape[1]
    FT = F // P
    LEAD = KC + 2
    STACK = TERMS * DMA
    SCALE = float(D) ** -0.5

    HPT = H // CT
    PAIR = HG // CT

    def head(g, j):
        return j % CT * HPT + g * PAIR + j // CT

    r_dram = nc.dram_tensor("r_scratch", [B, C, T], F32, kind="Internal").ap()
    ctx_dram = nc.dram_tensor("ctx_scratch", [B, H, 2 * D, T], F32, kind="Internal").ap()
    inv_dram = nc.dram_tensor("inv_scratch", [B, H, T], F32, kind="Internal").ap()

    with ExitStack() as es:
        def sb(name, shape, dt=F32):
            return es.enter_context(nc.sbuf_tensor(name, shape, dt))

        def bank(name, shape=(P, 512)):
            return es.enter_context(nc.psum_tensor(name, list(shape), F32))

        def sem(name):
            return es.enter_context(nc.semaphore(name))

        ident = sb("ident", [P, P])
        neg_half = sb("neg_half", [P, KC])
        pe_tab = sb("pe_tab", [P, CT, T])
        w_split = {n: sb("w_split_" + n, [P, 2, CT, C], F32R) for n in "kqvo"}
        vecs = sb("vecs", [P, 10 * CT])
        b1_col = sb("b1_col", [P, FT])
        gq, bq, gk, bk, gf, bf, b2_col = (vecs[:, CT * i:CT * i + CT] for i in range(7))

        x_in = sb("x_in", [P, CT, T])
        kv_in = sb("kv_in", [P, CT, T])
        tok = {"k": sb("tok_k", [P, KC, C]), "q": sb("tok_q", [P, KC, C])}
        stat = {"k": sb("stat_k", [P, KC, 6]), "q": sb("stat_q", [P, KC, 6])}
        mv = {"k": sb("mv_k", [P, KC, 2]), "q": sb("mv_q", [P, KC, 2])}
        rstd = {"k": sb("rstd_k", [P, KC]), "q": sb("rstd_q", [P, KC])}
        ln = {"k": sb("ln_k", [P, CT, T]), "q": sb("ln_q", [P, CT, T])}
        ln_parts = {n: sb("ln_parts_" + n, [P, 2, CT, T], F32R) for n in "kq"}
        parts = sb("parts", [P, 4, CT, T], F32R)
        hi = {"k": parts[:, 0], "q": parts[:, 2]}
        lo = {"k": parts[:, 1], "q": parts[:, 3]}
        stacks = sb("stacks", [P, NG, 2, PAIR, CT, T], F32R)
        v_ones = sb("v_ones", [P, KC, H, 2 * D])
        probs = sb("probs", [P, 2, HG, T])
        neg_max = sb("neg_max", [P, 2, 2, HG * KC])
        m_hi = sb("m_hi", [2 * HG * KC, P], F32R)
        m_both = sb("m_both", [2 * HG * KC, P], F32R)
        lo_rows = sb("lo_rows", [2 * HG * KC, 1])
        pv_sb = sb("pv_sb", [P, 2, T])
        ctx_raw = sb("ctx_raw", [P, CT, T])
        ctx_parts = sb("ctx_parts", [P, 2, CT, T], F32R)
        sums = sb("sums", [P, H * T // P])
        inv_sum = sb("inv_sum", [P, CT, T])
        q_mid = sb("q_mid", [P, CT, T])
        q_res = sb("q_res", [P, CT, T])
        r_out = sb("r_out", [P, CT, T])
        r_buf = sb("r_buf", [P, 2, CT, T])

        sc_ps = [bank("sc_ps0"), bank("sc_ps1")]
        mx_ps = [bank("mx_ps0"), bank("mx_ps1")]
        pv_ps = bank("pv_ps")
        t_ps = [bank("t_ps0"), bank("t_ps1")]
        xc_ps = bank("xc_ps")

        consts = sem("consts")
        cleared = sem("cleared")
        table = sem("table")
        weights = sem("weights")
        ffw_weights = sem("ffw_weights")
        ffw_split = sem("ffw_split")
        w_hi_done = sem("w_hi_done")
        w_lo_done = sem("w_lo_done")
        loaded = {"k": sem("kv_loaded"), "q": sem("x_loaded")}
        pos_added = {"k": sem("kv_pos_added"), "q": sem("x_pos_added")}
        tr_in = {"k": sem("k_tr_in"), "q": sem("q_tr_in")}
        tok_ready = {"k": sem("k_tok"), "q": sem("q_tok")}
        bn_done = {"k": sem("k_bn"), "q": sem("q_bn")}
        stat_done = {"k": sem("k_stat"), "q": sem("q_stat")}
        rstd_step = {"k": sem("k_rstd"), "q": sem("q_rstd")}
        normed = {"k": sem("k_normed"), "q": sem("q_normed")}
        tr_out = {"k": sem("k_tr_out"), "q": sem("q_tr_out")}
        ln_done = {"k": sem("k_ln"), "q": sem("q_ln")}
        rounded = {"k": sem("k_ln_hi"), "q": sem("q_ln_hi")}
        rest_done = {"k": sem("k_ln_lo"), "q": sem("q_ln_lo")}
        proj = {"k": sem("k_proj"), "q": sem("q_proj")}
        hi_done = {"k": sem("k_hi"), "q": sem("q_hi")}
        lo_done = {"k": sem("k_lo"), "q": sem("q_lo")}
        stacked = [sem(f"stacked{g}_{i}") for g in range(NG) for i in range(PAIR)]
        v_made = sem("v_made")
        v_done = sem("v_done")
        mx_made = sem("mx_made")
        mx_done = sem("mx_done")
        mx_twice = sem("mx_twice")
        mt_made = sem("mt_made")
        mhi_done = sem("mhi_done")
        mlo_done = sem("mlo_done")
        m_placed = [sem(f"m_placed{g}") for g in range(NG)]
        sc_made = sem("sc_made")
        exp_done = sem("exp_done")
        pv_made = sem("pv_made")
        pv_out = sem("pv_out")
        pv_stored = [sem(f"pv_stored{g}") for g in range(NG)]
        sums_loaded = sem("sums_loaded")
        ctx_loaded = sem("ctx_loaded")
        inv_stored = sem("inv_stored")
        inv_loaded = sem("inv_loaded")
        inverted = sem("inverted")
        ctx_done = sem("ctx_done")
        ctx_rounded = sem("ctx_rounded")
        ctx_rest_done = sem("ctx_rest_done")
        wo_made = sem("wo_made")
        q_saved = sem("q_saved")
        q_kept = sem("q_kept")
        r_done = sem("r_done")
        r_stored = sem("r_stored")

        def wait_apart(eng, semaphore, value):
            if not isinstance(value, int):
                value = eng.to_reg(value)
            eng.wait_ge(consts, 1)
            eng.wait_ge(semaphore, value)

        def unit_of(b, s, j):
            return b * UNITS + s * HG + j

        qk_ps = {"k": t_ps[0], "q": t_ps[1]}
        src = {"k": kv_in, "q": x_in}
        gain, bias = {"k": gk, "q": gq}, {"k": bk, "q": bq}
        w_raw = {"k": q_mid[:, :, 0:C], "q": q_mid[:, :, C:2 * C], "v": r_out[:, :, 0:C],
                 "o": r_out[:, :, C:2 * C]}

        tok_f = tok["k"]
        stat_f, mv_f, rstd_f = stat["k"], mv["k"], rstd["k"]
        r_keep = [q_mid, kv_in]
        w_1, w_2 = x_in, kv_in[:, :, :].rearrange("p t (f c) -> p (t f) c", c=C)
        w1_split = [parts[:, i] for i in range(2)]
        w2_split = [parts[:, 2 + i].rearrange("p t (f c) -> p (t f) c", c=C) for i in range(2)]
        out_buf = x_in
        h_full, act_full = ln["k"], probs[:, 0]
        h_hi, h_lo = stacks[:, 0, 0, 0], stacks[:, 0, 1, 0]
        act_hi = [stacks[:, 1 + i, 0].rearrange("p i t n -> p (i t) n") for i in range(2)]
        act_lo = [stacks[:, 1 + i, 1].rearrange("p i t n -> p (i t) n") for i in range(2)]
        up_ps, down_ps = sc_ps + mx_ps, [pv_ps, xc_ps]

        r_loaded = [sem("r_loaded0"), sem("r_loaded1")]
        f_tr_in = sem("f_tr_in")
        f_tok = sem("f_tok")
        f_bn = sem("f_bn")
        f_stat = sem("f_stat")
        f_rstd = sem("f_rstd")
        f_kept = sem("f_kept")
        f_normed = sem("f_normed")
        f_tr_out = sem("f_tr_out")
        f_ln = sem("f_ln")
        h_split = sem("h_split")
        up_made = sem("up_made")
        gelu_done = sem("gelu_done")
        act_split = sem("act_split")
        down_made = sem("down_made")
        out_done = sem("out_done")
        out_stored = sem("out_stored")

        def zero(b):
            return isinstance(b, int) and b == 0

        def turns(eng, turn):
            turn(0, 0)
            turn(1, 1)
            with eng.Fori(1, B // 2 - 1) as i:
                turn(2 * i, 0)
                turn(2 * i + 1, 1)
            turn(B - 2, 0)
            turn(B - 1, 1)

        def is_last(b):
            return isinstance(b, int) and b == B - 1

        with nc.Block() as block:
            @block.sync
            def _(sp):
                def load(b, n):
                    if not (isinstance(b, int) and b == 0):
                        wait_apart(sp, tr_in[n], b * 2)
                    d = {"k": ctx_in, "q": x}[n]
                    sp.dma_start(src[n][:, :, :], d[b].rearrange("(t p) n -> p t n", p=P)
                                 ).then_inc(loaded[n], DMA)

                def fill_stack(b, g):
                    wait_apart(sp, lo_done["k"], b * 2 + 2)
                    wait_apart(sp, lo_done["q"], b * 2 + 2)
                    if not (isinstance(b, int) and b == 0):
                        wait_apart(sp, sc_made, unit_of(b, (g + 1) * KC, 0) - UNITS)
                    for i in range(PAIR):
                        rows = slice((g * PAIR + i) * D, (g * PAIR + i + 1) * D)
                        for kp in range(2):
                            for qp in range(2):
                                to = (2 * kp + qp) * D
                                sp.dma_start(stacks[to:to + D, g, :, i, :, :].bitcast(F32),
                                             parts[rows, kp:qp + 3:qp + 2 - kp, :, :].bitcast(F32)
                                             ).then_inc(stacked[PAIR * g + i], DMA)

                def store_pv(b, g):
                    wait_apart(sp, pv_out, b * NG + g + 1)
                    sp.dma_start(ctx_dram[b, g * HG:(g + 1) * HG].rearrange("h r n -> (h r) n"),
                                 pv_sb[:, g % 2, :]).then_inc(pv_stored[g], DMA)

                def load_ctx(b):
                    for g in range(NG):
                        wait_apart(sp, pv_stored[g], (b + 1) * DMA)
                    sp.dma_start(sums[:, :], ctx_dram[b, :, D, :].rearrange("h (a n) -> h a n", a=P // H)
                                 ).then_inc(sums_loaded, DMA)
                    if not (isinstance(b, int) and b == 0):
                        wait_apart(sp, wo_made, b * CT)
                    for t in range(CT):
                        sp.dma_start(ctx_raw[:, t, :], ctx_dram[b].rearrange("(h t) r n -> t h r n", t=CT)[t, :, 0:D, :]
                                     ).then_inc(ctx_loaded, DMA)

                def spread_inverse(b):
                    wait_apart(sp, inverted, b + 1)
                    sp.dma_start(inv_dram[b].rearrange("h (a n) -> h a n", a=P // H), sums[:, :]
                                 ).then_inc(inv_stored, DMA)
                    wait_apart(sp, inv_stored, (b + 1) * DMA)
                    for t in range(CT):
                        sp.dma_start(inv_sum[:, t, :], inv_dram[b].rearrange("(h t) n -> t h n", t=CT)[t]
                                     .unsqueeze(1).to_broadcast([HPT, D, T])).then_inc(inv_loaded, DMA)

                def store_r(b):
                    wait_apart(sp, r_done, b * CT + CT)
                    sp.dma_start(r_dram[b].rearrange("(t p) n -> p t n", p=P), r_out[:, :, :]
                                 ).then_inc(r_stored, DMA)

                def save_q(b):
                    wait_apart(sp, ln_done["q"], b * 2 + 2)
                    if not (isinstance(b, int) and b == 0):
                        wait_apart(sp, q_kept, b * DMA)
                    sp.dma_start(q_mid[:, :, :], ln["q"][:, :, :]).then_inc(q_saved, DMA)

                def keep_q(b):
                    wait_apart(sp, q_saved, b * DMA + DMA)
                    if not (isinstance(b, int) and b == 0):
                        wait_apart(sp, r_done, b * CT)
                    sp.dma_start(q_res[:, :, :], q_mid[:, :, :]).then_inc(q_kept, DMA)

                def load_r(b, i):
                    if not (isinstance(b, int) and b < 2):
                        wait_apart(sp, f_tr_in, b * 2 - 2)
                        wait_apart(sp, f_kept, b - 1)
                    if isinstance(b, int) and b == 3:
                        wait_apart(sp, r_stored, B * DMA)
                    sp.dma_start(r_buf[:, i, :, :], r_dram[b].rearrange("(t p) n -> p t n", p=P)
                                 ).then_inc(r_loaded[i], DMA)

                def store(b):
                    wait_apart(sp, out_done, b * CT + CT)
                    sp.dma_start(out[b].rearrange("(t p) n -> p t n", p=P), out_buf[:, :, :]
                                 ).then_inc(out_stored, DMA)

                def batch(b, first=False, last=False, load_more=True):
                    fill_stack(b, NG - 1)
                    if not first:
                        store_pv(b - 1, NG - 1)
                        load_ctx(b - 1)
                    if load_more:
                        load(b + 2, "k")
                        load(b + 2, "q")
                    if not first:
                        spread_inverse(b - 1)
                    store_pv(b, 0)
                    if not last:
                        fill_stack(b + 1, 0)
                    store_pv(b, 1)
                    if not last:
                        fill_stack(b + 1, 1)
                        fill_stack(b + 1, 2)
                    if not first:
                        store_r(b - 1)
                    keep_q(b)
                    if not last:
                        save_q(b + 1)
                    store_pv(b, 2)

                load(0, "k")
                sp.dma_start(pe_tab[:, :, :], pos.rearrange("(t p) n -> p t n", p=P)).then_inc(table, DMA)
                load(0, "q")
                load(1, "k")
                load(1, "q")
                for g in range(NG - 1):
                    fill_stack(0, g)
                sp.wait_ge(w_lo_done, 4)
                save_q(0)
                batch(0, first=True)
                with sp.Fori(1, B - 2) as b:
                    batch(b)
                batch(B - 2, load_more=False)
                sp.wait_ge(r_stored, (B - 2) * DMA)
                load_r(0, 0)
                load_r(1, 1)
                sp.wait_ge(tr_in["k"], B * 2)
                sp.wait_ge(tr_in["q"], B * 2)
                sp.dma_start(w_1[:, :, :], W1.rearrange("(t p) n -> p t n", p=P)).then_inc(ffw_weights, DMA)
                sp.dma_start(w_2, W2.rearrange("(t p) n -> p t n", p=P)).then_inc(ffw_weights, DMA)
                sp.dma_start(b1_col[:, :], b1.rearrange("(t p) -> p t", p=P),
                             allow_slow_non_contiguous=True).then_inc(ffw_weights, DMA)
                batch(B - 1, last=True, load_more=False)
                load_r(2, 0)
                store_pv(B - 1, NG - 1)
                load_ctx(B - 1)
                spread_inverse(B - 1)
                store_r(B - 1)
                load_r(3, 1)
                store(0)
                with sp.Fori(1, B // 2 - 1) as i:
                    load_r(2 * i + 2, 0)
                    store(2 * i - 1)
                    load_r(2 * i + 3, 1)
                    store(2 * i)
                store(B - 3)
                store(B - 2)
                store(B - 1)
                sp.wait_ge(r_stored, B * DMA)
                sp.wait_ge(out_stored, B * DMA)

            @block.gpsimd
            def _(pool):
                def add_pos(b, n):
                    pool.wait_ge(loaded[n], b * DMA + DMA)
                    pool.tensor_tensor(src[n][:, :, :], src[n][:, :, :], pe_tab[:, :, :], ALU.add
                                       ).then_inc(pos_added[n], 1)

                def inv_std(b, n):
                    wait_apart(pool, stat_done[n], b * KC + KC)
                    pool.tensor_scalar(rstd[n][:, :], mv[n][:, :, 1], EPS, None, ALU.add
                                       ).then_inc(rstd_step[n], 1)
                    pool.wait_ge(rstd_step[n], b * 2 + 1)
                    pool.tensor_tensor(rstd[n][:, :], rstd[n][:, :], neg_half[:, :], ALU.pow
                                       ).then_inc(rstd_step[n], 1)

                def normalise(b, n):
                    wait_apart(pool, rstd_step[n], b * 2 + 2)
                    for c in range(KC):
                        pool.tensor_scalar(tok[n][:, c, :], tok[n][:, c, :], mv[n][:, c, 0:1],
                                           rstd[n][:, c:c + 1], ALU.subtract, ALU.mult
                                           ).then_inc(normed[n], 1)

                def ln_rest(b, n, t):
                    wait_apart(pool, rounded[n], b * 2 + t + 1)
                    pool.tensor_tensor(ln_parts[n][:, 1, t, :], ln[n][:, t, :],
                                       ln_parts[n][:, 0, t, :].bitcast(F32), ALU.subtract
                                       ).then_inc(rest_done[n], 1)

                def ctx_rest(b):
                    for t in range(CT):
                        wait_apart(pool, ctx_rounded, b * CT + t + 1)
                        pool.tensor_tensor(ctx_parts[:, 1, t, :], ctx_raw[:, t, :],
                                           ctx_parts[:, 0, t, :].bitcast(F32), ALU.subtract
                                           ).then_inc(ctx_rest_done, 1)

                def tokens(b):
                    inv_std(b, "k")
                    normalise(b, "k")
                    inv_std(b, "q")

                pool.memset(ident[:, :], 0.0).then_inc(consts, 1)
                pool.memset(neg_half[:, :], -0.5).then_inc(consts, 1)
                pool.wait_ge(consts, 2)
                pool.affine_select(out=ident[:, :], in_=ident[:, :], compare_op=ALU.not_equal, fill=1.0,
                                   base=0, pattern=[[-1, P]], channel_multiplier=1).then_inc(consts, 1)
                pool.wait_ge(consts, 3)
                pool.memset(lo_rows[:, :], -1.0).then_inc(consts, 1)
                pool.wait_ge(consts, 4)
                pool.memset(lo_rows[0:HG * KC, :], 0.0).then_inc(consts, 1)
                pool.wait_ge(consts, 5)
                pool.memset(v_ones[:, :, :, D:2 * D], 1.0).then_inc(consts, 1)
                pool.wait_ge(consts, 6)
                pool.memset(stacks[REST:P, 0, 1].bitcast(F32), 0.0).then_inc(cleared, 1)
                pool.memset(stacks[REST:P, 0:2, 0].bitcast(F32), 1.0).then_inc(cleared, 1)
                pool.wait_ge(cleared, 2)
                inv_std(0, "k")
                inv_std(0, "q")
                for n in "kq":
                    for t in range(CT):
                        ln_rest(0, n, t)
                pool.wait_ge(rest_done["q"], 2)
                pool.memset(stacks[REST:P, 2:NG, 0].bitcast(F32), 1.0).then_inc(cleared, 1)
                pool.wait_ge(cleared, 3)
                add_pos(1, "k")
                add_pos(1, "q")
                pool.wait_ge(pos_added["q"], 2)
                pool.memset(stacks[REST:P, 1:NG, 1].bitcast(F32), 0.0).then_inc(cleared, 1)
                pool.wait_ge(cleared, 4)
                tokens(1)
                def ln_rests(b):
                    for n in "kq":
                        for t in range(CT):
                            ln_rest(b, n, t)

                def batch(b, first=False):
                    ln_rests(b + 1)
                    add_pos(b + 2, "k")
                    add_pos(b + 2, "q")
                    if not first:
                        ctx_rest(b - 1)
                    tokens(b + 2)

                batch(0, first=True)
                with pool.Fori(1, B - 2) as b:
                    batch(b)
                ln_rests(B - 1)
                ctx_rest(B - 3)
                ctx_rest(B - 2)
                for pair in stacked:
                    pool.wait_ge(pair, B * STACK)
                pool.wait_ge(ffw_weights, 3 * DMA)
                splits = ((w_1[:, :, :], w1_split), (w_2, w2_split))
                for full, split in splits:
                    pool.tensor_copy(split[0], full).then_inc(ffw_split, 1)
                for n, (full, split) in enumerate(splits):
                    pool.wait_ge(ffw_split, n + 1)
                    pool.tensor_tensor(split[1], full, split[0].bitcast(F32), ALU.subtract
                                       ).then_inc(ffw_split, 1)
                pool.wait_ge(q_kept, B * DMA)

                def inv_std_f(b):
                    wait_apart(pool, f_stat, b * KC + KC)
                    if not zero(b):
                        pool.wait_ge(f_normed, b * KC)
                    pool.tensor_scalar(rstd_f[:, :], mv_f[:, :, 1], EPS, None, ALU.add).then_inc(f_rstd, 1)
                    pool.wait_ge(f_rstd, b * 2 + 1)
                    pool.tensor_tensor(rstd_f[:, :], rstd_f[:, :], neg_half[:, :], ALU.pow
                                       ).then_inc(f_rstd, 1)

                def keep_r(b, i):
                    if not (isinstance(b, int) and b < 2):
                        wait_apart(pool, out_done, b * CT - CT)
                    wait_apart(pool, r_loaded[i], (b - i) * (DMA // 2) + DMA)
                    pool.tensor_copy(r_keep[i][:, :, :], r_buf[:, i, :, :]).then_inc(f_kept, 1)

                def turn(b, i):
                    inv_std_f(b)
                    keep_r(b, i)
                    if isinstance(b, int) and b == 1:
                        ctx_rest(B - 1)

                turns(pool, turn)

            @block.scalar
            def _(act):
                def take_tok(b, n, half):
                    act.wait_ge(tr_in[n], b * 2 + half + 1)
                    if half == 0 and not (isinstance(b, int) and b == 0):
                        act.wait_ge(tr_out[n], b * 2)
                    act.activation(tok[n][:, 2 * half:2 * half + 2, :], t_ps[half][:, :], ACT.Copy
                                   ).then_inc(tok_ready[n], 1)

                def take_ln(b, n, t):
                    act.wait_ge(tr_out[n], b * 2 + t + 1)
                    if t == 0 and not (isinstance(b, int) and b == 0):
                        act.wait_ge(rest_done[n], b * 2)
                        if n == "q":
                            act.wait_ge(q_saved, b * DMA)
                    act.activation(ln[n][:, t, :], t_ps[t][:, :], ACT.Identity,
                                   scale=gain[n][:, t:t + 1], bias=bias[n][:, t:t + 1]
                                   ).then_inc(ln_done[n], 1)

                def round_ln(b, n, t):
                    act.wait_ge(ln_done[n], b * 2 + t + 1)
                    if t == 0 and not (isinstance(b, int) and b == 0):
                        act.wait_ge(proj[n], b * 2)
                        if n == "k":
                            act.wait_ge(v_made, b * KC)
                    act.activation(ln_parts[n][:, 0, t, :], ln[n][:, t, :], ACT.Copy).then_inc(rounded[n], 1)

                def round_ctx(b, t):
                    act.wait_ge(ctx_done, b * CT + t + 1)
                    act.activation(ctx_parts[:, 0, t, :], ctx_raw[:, t, :], ACT.Copy).then_inc(ctx_rounded, 1)

                def take_hi(b, n, t):
                    act.wait_ge(proj[n], b * 2 + t + 1)
                    if not (isinstance(b, int) and b == 0):
                        if n == "k" and t == 0:
                            for pair in stacked:
                                act.wait_ge(pair, b * STACK)
                    act.activation(hi[n][:, t, :], qk_ps[n][:, :], ACT.Copy).then_inc(hi_done[n], 1)

                def take_v(b, c):
                    act.wait_ge(v_made, b * KC + c + 1)
                    if not (isinstance(b, int) and b == 0):
                        act.wait_ge(pv_made, b * STEPS + c + 1 - KC)
                    act.activation(v_ones[:, c, :, 0:D],
                                   xc_ps[:, 0:C].rearrange("p (h d) -> p h d", d=D), ACT.Copy
                                   ).then_inc(v_done, 1)

                def exp(b, s, j, first=False):
                    act.wait_ge(sc_made, unit_of(b, s, j) + 1)
                    if j == 0 and not (first and s < 2):
                        act.wait_ge(pv_made, b * STEPS + s - 1)
                    act.activation(probs[:, s % 2, j, :], sc_ps[j % 2][:, :], ACT.Exp, scale=SCALE
                                   ).then_inc(exp_done, 1)

                def place_max(b, g):
                    act.wait_ge(mlo_done, b * NG + g + 1)
                    act.dma_start(stacks[MROW:MROW + 2, g, 1, :, :, :].bitcast(F32),
                                 m_both[:, :].bitcast(F32)).then_inc(m_placed[g], DMA)

                def take_pv(b, g, first=False):
                    act.wait_ge(pv_made, b * STEPS + (g + 1) * KC)
                    if g >= 2:
                        act.wait_ge(pv_stored[g - 2], (b + 1) * DMA)
                    elif not first:
                        act.wait_ge(pv_stored[g + 2], b * DMA)
                    act.activation(pv_sb[:, g % 2, :], pv_ps[:, :], ACT.Copy).then_inc(pv_out, 1)

                def take_tok_f(b, half):
                    act.wait_ge(f_tr_in, b * 2 + half + 1)
                    if half == 0 and not zero(b):
                        act.wait_ge(f_tr_out, b * 2)
                    act.activation(tok_f[:, 2 * half:2 * half + 2, :], t_ps[half][:, :], ACT.Copy
                                   ).then_inc(f_tok, 1)

                def take_ln_f(b):
                    for t in range(CT):
                        act.wait_ge(f_tr_out, b * 2 + t + 1)
                        act.activation(h_hi[:, t, :], t_ps[t][:, :], ACT.Identity,
                                       scale=gf[:, t:t + 1], bias=bf[:, t:t + 1]).then_inc(f_ln, 1)
                    if not zero(b):
                        act.wait_ge(h_split, b * CT)
                    for t in range(CT):
                        act.activation(h_full[:, t, :], t_ps[t][:, :], ACT.Identity,
                                       scale=gf[:, t:t + 1], bias=bf[:, t:t + 1]).then_inc(f_ln, 1)

                def gelu(b, i, f):
                    act.wait_ge(up_made, b * FT + f + 1)
                    if f == 0 and not (isinstance(b, int) and b < 2):
                        act.wait_ge(down_made, b * CT - CT)
                    act.activation(act_hi[i][:, f, :], up_ps[f][:, :], ACT.Gelu,
                                   bias=b1_col[:, f:f + 1]).then_inc(gelu_done, 1)
                    if not zero(b):
                        act.wait_ge(act_split, b * FT - FT + f + 1)
                    act.activation(act_full[:, f, :], up_ps[f][:, :], ACT.Gelu,
                                   bias=b1_col[:, f:f + 1]).then_inc(gelu_done, 1)

                def turn(b, i):
                    gelu(b, i, 0)
                    if not is_last(b):
                        take_tok_f(b + 1, 0)
                        take_tok_f(b + 1, 1)
                    gelu(b, i, 1)
                    gelu(b, i, 2)
                    if not is_last(b):
                        take_ln_f(b + 1)
                    gelu(b, i, 3)
                    if zero(b):
                        round_ctx(B - 1, 0)
                        round_ctx(B - 1, 1)

                def batch(b, first=False, last=False, more=True):
                    for s in range(STEPS):
                        exp(b, s, 0, first)
                        if last and s == 13:
                            take_tok_f(0, 0)
                            take_tok_f(0, 1)
                        if not last:
                            if s == 3:
                                take_ln(b + 1, "q", 0)
                            if s == 4:
                                round_ln(b + 1, "q", 1)
                            if s == 6:
                                take_hi(b + 1, "k", 1)
                            if s in (5, 7):
                                take_hi(b + 1, "q", s // 6)
                            if s == 14:
                                take_v(b + 1, 0)
                        if s in (0, 1) and not first:
                            take_v(b, s + 1)
                        if s == 2:
                            take_v(b, 3)
                        if more and s in (10, 11, 12, 13):
                            take_tok(b + 2, "k" if s < 12 else "q", s % 2)
                        exp(b, s, 1, first)
                        if s % KC == 3 and s + 1 < STEPS:
                            place_max(b, (s + 1) // KC)
                        elif s % KC == 3 and not last:
                            place_max(b + 1, 0)
                        if not last:
                            if s == 1:
                                take_ln(b + 1, "k", 1)
                            if s == 2:
                                round_ln(b + 1, "k", 0)
                            if s == 3:
                                take_ln(b + 1, "q", 1)
                            if s == 4:
                                take_hi(b + 1, "k", 0)
                        if s in (5, 6) and not first:
                            round_ctx(b - 1, s - 5)
                        exp(b, s, 2, first)
                        if s % KC == 0 and s:
                            take_pv(b, s // KC - 1, first)
                        if s == 0 and not first:
                            take_pv(b - 1, NG - 1)
                        exp(b, s, 3, first)
                        if not last:
                            if s == 0:
                                take_ln(b + 1, "k", 0)
                            if s == 2:
                                round_ln(b + 1, "k", 1)
                            if s == 3:
                                round_ln(b + 1, "q", 0)

                act.dma_start(w_raw["k"], Wk.rearrange("(t p) n -> p t n", p=P)).then_inc(weights, DMA)
                act.dma_start(w_raw["q"], Wq.rearrange("(t p) n -> p t n", p=P)).then_inc(weights, DMA)
                act.dma_start(w_raw["v"], Wv.rearrange("(t p) n -> p t n", p=P)).then_inc(weights, DMA)
                act.dma_start(w_raw["o"], Wo.rearrange("(t p) n -> p t n", p=P)).then_inc(weights, DMA)
                for dst, v in ((gq, ln_q_g), (bq, ln_q_b), (gk, ln_kv_g), (bk, ln_kv_b),
                               (gf, ffn_g), (bf, ffn_b), (b2_col, b2)):
                    act.dma_start(dst, v.rearrange("(t p) -> p t", p=P),
                                  allow_slow_non_contiguous=True).then_inc(weights, DMA)
                for n in "kq":
                    for half in range(2):
                        take_tok(0, n, half)
                act.wait_ge(weights, 11 * DMA)
                for n in "kqvo":
                    act.activation(w_split[n][:, 0], w_raw[n], ACT.Copy).then_inc(w_hi_done, 1)
                for n in "kq":
                    for t in range(CT):
                        take_ln(0, n, t)
                    for t in range(CT):
                        round_ln(0, n, t)
                for t in range(CT):
                    for n in "kq":
                        take_hi(0, n, t)
                for c in range(3):
                    take_v(0, c)
                    if c < 2:
                        take_tok(1, "k", c)
                for half in range(2):
                    take_tok(1, "q", half)
                place_max(0, 0)
                batch(0, first=True)
                with act.Fori(1, B - 2) as b:
                    batch(b)
                batch(B - 2, more=False)
                batch(B - 1, last=True, more=False)
                take_pv(B - 1, NG - 1)
                act.wait_ge(ffw_weights, 3 * DMA)
                take_ln_f(0)
                turns(act, turn)

            @block.vector
            def _(dve):
                def token_stats(b, n, c):
                    dve.wait_ge(tok_ready[n], b * 2 + c // 2 + 1)
                    dve.bn_stats(stat[n][:, c, :], tok[n][:, c, :]).then_inc(bn_done[n], 1)

                def mean_var(b, n):
                    if not (isinstance(b, int) and b == 0):
                        wait_apart(dve, normed[n], b * KC)
                    wait_apart(dve, bn_done[n], b * KC + KC)
                    for c in range(KC):
                        dve.bn_aggr(mv[n][:, c, :], stat[n][:, c, :]).then_inc(stat_done[n], 1)

                def normalise(b, n, c):
                    dve.wait_ge(rstd_step[n], b * 2 + 2)
                    dve.tensor_scalar(tok[n][:, c, :], tok[n][:, c, :], mv[n][:, c, 0:1],
                                      rstd[n][:, c:c + 1], ALU.subtract, ALU.mult
                                      ).then_inc(normed[n], 1)

                def take_lo(b, n, t):
                    dve.wait_ge(hi_done[n], b * 2 + t + 1)
                    dve.tensor_tensor(lo[n][:, t, :], qk_ps[n][:, :], hi[n][:, t, :].bitcast(F32),
                                      ALU.subtract).then_inc(lo_done[n], 1)

                def row_max(b, q, j, first=False, fresh=False):
                    g, c = q // KC, q % KC
                    dve.wait_ge(mx_made, unit_of(b, q, j) + 1)
                    if c == 0 and j == 0 and not (first and g < 2):
                        dve.wait_ge(mt_made, b * NG + g - 1)
                    source = (mx_ps + sc_ps)[j] if fresh else mx_ps[j % 2]
                    dve.tensor_reduce(neg_max[:, g % 2, 0, j * KC + c:j * KC + c + 1], source[:, :],
                                      AX_X, ALU.max, negate=True).then_inc(mx_done, 1)

                def repeat_max(b, g):
                    dve.wait_ge(mx_done, unit_of(b, (g + 1) * KC, 0))
                    dve.tensor_copy(neg_max[:, g % 2, 1, :], neg_max[:, g % 2, 0, :]).then_inc(mx_twice, 1)

                def max_hi(b, g):
                    dve.wait_ge(mt_made, b * NG + g + 1)
                    if not (isinstance(b, int) and b == 0 and g == 0):
                        dve.wait_ge(mlo_done, b * NG + g)
                    dve.tensor_copy(m_hi[:, :], xc_ps[0:2 * HG * KC, 0:P]).then_inc(mhi_done, 1)

                def split_max(b, g, first=False):
                    if g >= 1:
                        dve.wait_ge(m_placed[g - 1], b * DMA + DMA)
                    elif not first:
                        dve.wait_ge(m_placed[NG - 1], b * DMA)
                    dve.wait_ge(mhi_done, b * NG + g + 1)
                    dve.scalar_tensor_tensor(m_both[:, :], m_hi[:, :].bitcast(F32), lo_rows[:, 0:1],
                                             xc_ps[0:2 * HG * KC, 0:P], ALU.mult, ALU.add
                                             ).then_inc(mlo_done, 1)

                def invert_sums(b):
                    dve.wait_ge(sums_loaded, b * DMA + DMA)
                    dve.reciprocal(sums[:, :], sums[:, :]).then_inc(inverted, 1)

                def scale_ctx(b, t):
                    dve.wait_ge(ctx_loaded, (b + 1) * 2 * DMA)
                    dve.wait_ge(inv_loaded, (b + 1) * 2 * DMA)
                    dve.tensor_tensor(ctx_raw[:, t, :], ctx_raw[:, t, :], inv_sum[:, t, :], ALU.mult
                                      ).then_inc(ctx_done, 1)

                def add_q(b, t):
                    dve.wait_ge(wo_made, b * CT + t + 1)
                    if t == 0:
                        dve.wait_ge(q_kept, b * DMA + DMA)
                        if not (isinstance(b, int) and b == 0):
                            dve.wait_ge(r_stored, b * DMA)
                    dve.tensor_tensor(r_out[:, t, :], xc_ps[:, :], q_res[:, t, :], ALU.add
                                      ).then_inc(r_done, 1)

                def tokens(b, s, j):
                    if (s, j) in STATS_K:
                        token_stats(b, "k", STATS_K.index((s, j)))
                    if (s, j) in STATS_Q:
                        token_stats(b, "q", STATS_Q.index((s, j)))
                    if (s, j) in ((2, 3), (5, 3)):
                        mean_var(b, "k" if s == 2 else "q")

                STATS_K = ((0, 1), (1, 1), (1, 3), (2, 1))
                STATS_Q = ((3, 1), (3, 3), (4, 1), (5, 1))

                def batch(b, first=False, last=False, more=True):
                    for s in range(STEPS):
                        q = s + LEAD
                        nb, nq = (b, q) if q < STEPS else (b + 1, q - STEPS)
                        for j in range(HG):
                            if q < STEPS or not last:
                                row_max(nb, nq, j, first and q < STEPS)
                            if q % KC == KC - 1 and j == HG - 1 and (q < STEPS or not last):
                                repeat_max(nb, nq // KC)
                            if not last:
                                if s < 2 and j in (1, 3):
                                    normalise(b + 1, "q", 2 * s + j // 2)
                                if (s, j) in ((4, 3), (6, 1)):
                                    take_lo(b + 1, "k", s // 5)
                                if s in (5, 7) and j == 1:
                                    take_lo(b + 1, "q", s // 6)
                            if more:
                                tokens(b + 2, s - 10, j)
                            if not first:
                                if (s, j) == (2, 1):
                                    invert_sums(b - 1)
                                if (s, j) in ((4, 1), (5, 3)):
                                    scale_ctx(b - 1, s - 4)
                                if s in (8, 9) and j == 1:
                                    add_q(b - 1, s - 8)
                            if s % KC == 2 and (s + 2 < STEPS or not last):
                                m = (b, (s + 2) // KC) if s + 2 < STEPS else (b + 1, 0)
                                if j == 2:
                                    max_hi(*m)
                                if j == 3:
                                    split_max(*m)

                for n in "kq":
                    dve.wait_ge(table, DMA)
                    dve.wait_ge(loaded[n], DMA)
                    dve.tensor_tensor(src[n][:, :, :], src[n][:, :, :], pe_tab[:, :, :], ALU.add
                                      ).then_inc(pos_added[n], 1)
                for n in "kq":
                    for c in range(KC):
                        token_stats(0, n, c)
                    mean_var(0, n)
                for n in "kq":
                    for c in range(KC):
                        normalise(0, n, c)
                for i, n in enumerate("kqvo"):
                    dve.wait_ge(w_hi_done, i + 1)
                    dve.tensor_tensor(w_split[n][:, 1], w_raw[n], w_split[n][:, 0].bitcast(F32), ALU.subtract
                                      ).then_inc(w_lo_done, 1)
                for t in range(CT):
                    for n in "kq":
                        take_lo(0, n, t)
                for q in range(LEAD):
                    for j in range(HG):
                        row_max(0, q, j, True, fresh=True)
                        if (q, j) == (KC, 1):
                            max_hi(0, 0)
                            split_max(0, 0, True)
                        tokens(1, q, j)
                    if q == KC - 1:
                        repeat_max(0, 0)

                batch(0, first=True)
                with dve.Fori(1, B - 2) as b:
                    batch(b)
                batch(B - 2, more=False)
                batch(B - 1, last=True, more=False)

                def stats_f(b):
                    for c in range(KC):
                        dve.wait_ge(f_tok, b * 2 + c // 2 + 1)
                        dve.bn_stats(stat_f[:, c, :], tok_f[:, c, :]).then_inc(f_bn, 1)
                    for c in range(KC):
                        wait_apart(dve, f_bn, b * KC + c + 1)
                        dve.bn_aggr(mv_f[:, c, :], stat_f[:, c, :]).then_inc(f_stat, 1)

                def normalise_f(b):
                    dve.wait_ge(f_rstd, b * 2 + 2)
                    for c in range(KC):
                        dve.tensor_scalar(tok_f[:, c, :], tok_f[:, c, :], mv_f[:, c, 0:1],
                                          rstd_f[:, c:c + 1], ALU.subtract, ALU.mult
                                          ).then_inc(f_normed, 1)

                def h_rest(b):
                    for t in range(CT):
                        dve.wait_ge(f_ln, b * 2 * CT + CT + t + 1)
                        dve.tensor_tensor(h_lo[:, t, :], h_full[:, t, :], h_hi[:, t, :].bitcast(F32),
                                          ALU.subtract).then_inc(h_split, 1)

                def act_rest(b, i, f):
                    dve.wait_ge(gelu_done, (b * FT + f) * 2 + 2)
                    dve.tensor_tensor(act_lo[i][:, f, :], act_full[:, f, :], act_hi[i][:, f, :].bitcast(F32),
                                      ALU.subtract).then_inc(act_split, 1)

                def finish(b, i, t):
                    dve.wait_ge(down_made, b * CT + t + 1)
                    if t == 0 and not zero(b):
                        dve.wait_ge(out_stored, b * DMA)
                    if t == 0:
                        dve.wait_ge(f_kept, b + 1)
                    dve.scalar_tensor_tensor(out_buf[:, t, :], down_ps[t][:, :], b2_col[:, t:t + 1],
                                             r_keep[i][:, t, :], ALU.add, ALU.add).then_inc(out_done, 1)

                def turn(b, i):
                    act_rest(b, i, 0)
                    if not is_last(b):
                        stats_f(b + 1)
                    act_rest(b, i, 1)
                    if zero(b):
                        invert_sums(B - 1)
                    else:
                        if isinstance(b, int) and b == 1:
                            add_q(B - 1, 0)
                        finish(b - 1, 1 - i, 0)
                    if not is_last(b):
                        normalise_f(b + 1)
                    act_rest(b, i, 2)
                    if isinstance(b, int) and b == 1:
                        add_q(B - 1, 1)
                    if not is_last(b):
                        h_rest(b + 1)
                    if zero(b):
                        scale_ctx(B - 1, 0)
                        scale_ctx(B - 1, 1)
                    else:
                        finish(b - 1, 1 - i, 1)
                    act_rest(b, i, 3)

                stats_f(0)
                normalise_f(0)
                h_rest(0)
                turns(dve, turn)
                finish(B - 1, 1, 0)
                finish(B - 1, 1, 1)

            @block.tensor
            def _(pe):
                def transpose_in(b, n, half):
                    if half == 0:
                        pe.wait_ge(pos_added[n], b + 1)
                    if n == "q":
                        pe.wait_ge(tok_ready["k"], b * 2 + half + 1)
                    elif not (isinstance(b, int) and b == 0):
                        pe.wait_ge(lo_done["kq"[half]], b * 2)
                    for c in range(2):
                        for t in range(CT):
                            at = c * C + t * P
                            m = pe.transpose(t_ps[half][:, at:at + P],
                                             src[n][:, t, (2 * half + c) * P:(2 * half + c + 1) * P],
                                             ident[:, :])
                    m.then_inc(tr_in[n], 1)

                def transpose_out(b, n, t):
                    if t == 0:
                        pe.wait_ge(normed[n], b * KC + KC)
                    if n == "k":
                        pe.wait_ge(tok_ready["q"], b * 2 + t + 1)
                    else:
                        pe.wait_ge(ln_done["k"], b * 2 + t + 1)
                    for c in range(KC):
                        m = pe.transpose(t_ps[t][:, c * P:(c + 1) * P], tok[n][:, c, t * P:(t + 1) * P],
                                         ident[:, :])
                    m.then_inc(tr_out[n], 1)

                TERMS_3 = ((0, 0), (0, 1), (1, 0))

                def project(b, n, t):
                    if t == 0:
                        pe.wait_ge(rounded[n], b * 2 + 2)
                    if t == 1:
                        pe.wait_ge(lo_done[n], b * 2 + 1)
                    elif n == "k":
                        pe.wait_ge(ln_done["q"], b * 2 + 1)
                    cols = slice(t * P, (t + 1) * P)
                    for k in range(CT):
                        for part in (0, 1):
                            pe.matmul(qk_ps[n][:, :], w_split[n][:, part, k, cols], ln_parts[n][:, 0, k, :],
                                      start=(k + part == 0), stop=False)
                    if t == 0:
                        pe.wait_ge(rest_done[n], b * 2 + 2)
                    for k in range(CT):
                        m = pe.matmul(qk_ps[n][:, :], w_split[n][:, 0, k, cols], ln_parts[n][:, 1, k, :],
                                      start=False, stop=(k == CT - 1))
                    m.then_inc(proj[n], 1)

                def make_v(b, c):
                    if c == 0:
                        pe.wait_ge(ln_done["k"], b * 2 + 2)
                        if not (isinstance(b, int) and b == 0):
                            pe.wait_ge(mlo_done, b * NG)
                    elif c == 1 and not (isinstance(b, int) and b == 0):
                        pe.wait_ge(mlo_done, b * NG + 1)
                    elif c == 3 and isinstance(b, int) and b == 0:
                        pe.wait_ge(mlo_done, 1)
                    else:
                        pe.wait_ge(v_done, b * KC + c)
                    for i, (part, w_part) in enumerate(TERMS_3):
                        for k in range(CT):
                            m = pe.matmul(xc_ps[:, 0:C], ln_parts["k"][:, part, k, c * P:(c + 1) * P],
                                          w_split["v"][:, w_part, k, :],
                                          start=(i + k == 0), stop=(i == 2 and k == CT - 1))
                    m.then_inc(v_made, 1)

                def transpose_max(b, g, first=False, last=False):
                    pe.wait_ge(mx_twice, b * NG + g + 1)
                    if g == 0:
                        pe.wait_ge(v_done, b * KC + (3 if first else 1))
                    elif g == 1:
                        pe.wait_ge(v_done, b * KC + KC)
                    elif g == 3 and not first:
                        pe.wait_ge(r_done, b * CT)
                    else:
                        pe.wait_ge(mlo_done, b * NG + g)
                    pe.transpose(xc_ps[0:2 * HG * KC, 0:P], neg_max[:, g % 2, :, :], ident[:, :]
                                 ).then_inc(mt_made, 1)

                def max_scores(b, q, j, fresh=False):
                    g, c = q // KC, q % KC
                    if c == 0 and j % CT == 0:
                        pe.wait_ge(stacked[PAIR * g + j // CT], b * STACK + STACK)
                    if not fresh:
                        pe.wait_ge(mx_done, unit_of(b, q, j) - 1)
                    elif q:
                        pe.wait_ge(mx_done, unit_of(b, q, j) - 3)
                    target = (mx_ps + sc_ps)[j] if fresh else mx_ps[j % 2]
                    k_rows, q_rows = (stacks[0:MROW, g, n, j // CT, j % CT, :] for n in (0, 1))
                    pe.matmul(target[:, :], q_rows[:, c * P:(c + 1) * P], k_rows,
                              start=True, stop=True).then_inc(mx_made, 1)

                def scores(b, s, j, first=False):
                    g, c = s // KC, s % KC
                    if c == 0 and j == 0:
                        pe.wait_ge(m_placed[g], b * DMA + DMA)
                    if first and s == 0 and j < 2:
                        pe.wait_ge(mx_done, LEAD * HG)
                    else:
                        pe.wait_ge(exp_done, unit_of(b, s, j) - 1)
                    k_rows, q_rows = (stacks[:, g, n, j // CT, j % CT, :] for n in (0, 1))
                    pe.matmul(sc_ps[j % 2][:, :], k_rows[:, c * P:(c + 1) * P], q_rows,
                              start=True, stop=True).then_inc(sc_made, 1)

                def prob_value(b, s, first=False):
                    g, c = s // KC, s % KC
                    pe.wait_ge(exp_done, unit_of(b, s + 1, 0))
                    pe.wait_ge(v_done, b * KC + c + 1)
                    if c == 0 and not (first and g == 0):
                        pe.wait_ge(pv_out, b * NG + g)
                    for j in range(HG):
                        m = pe.matmul(pv_ps[32 * j:32 * j + 32, :], v_ones[:, c, head(g, j), :],
                                      probs[:, s % 2, j, :], start=(c == 0), stop=(c == KC - 1))
                    m.then_inc(pv_made, 1)

                def transpose_in_f(b, i, half):
                    if half == 0:
                        pe.wait_ge(r_loaded[i], (b - i) * (DMA // 2) + DMA)
                        if not zero(b):
                            pe.wait_ge(f_ln, b * 2 * CT)
                    for c in range(2):
                        for t in range(CT):
                            at = c * C + t * P
                            m = pe.transpose(t_ps[half][:, at:at + P],
                                             r_buf[:, i, t, (2 * half + c) * P:(2 * half + c + 1) * P],
                                             ident[:, :])
                    m.then_inc(f_tr_in, 1)

                def transpose_out_f(b, t):
                    if t == 0:
                        pe.wait_ge(f_normed, b * KC + KC)
                        pe.wait_ge(f_tok, b * 2 + 2)
                    for c in range(KC):
                        m = pe.transpose(t_ps[t][:, c * P:(c + 1) * P], tok_f[:, c, t * P:(t + 1) * P],
                                         ident[:, :])
                    m.then_inc(f_tr_out, 1)

                def up(b, f):
                    if f == 0:
                        pe.wait_ge(f_ln, b * 2 * CT + CT)
                    if not zero(b):
                        pe.wait_ge(gelu_done, (b * FT - FT + f) * 2 + 2)
                    cols = slice(f * P, (f + 1) * P)
                    for k in range(CT):
                        for part in (0, 1):
                            pe.matmul(up_ps[f][:, :], w1_split[part][:, k, cols], h_hi[:, k, :],
                                      start=(k + part == 0), stop=False)
                    for k in range(CT):
                        if f == 0:
                            pe.wait_ge(h_split, b * CT + k + 1)
                        m = pe.matmul(up_ps[f][:, :], w1_split[0][:, k, cols], h_lo[:, k, :],
                                      start=False, stop=(k == CT - 1))
                    m.then_inc(up_made, 1)

                def down(b, i, t):
                    if not zero(b):
                        pe.wait_ge(out_done, b * CT - CT + t + 1)
                    elif t == 0:
                        pe.wait_ge(pv_out, B * NG)
                    else:
                        pe.wait_ge(r_done, B * CT)
                    cols = slice(t * P, (t + 1) * P)
                    for f in range(FT):
                        if t == 0:
                            pe.wait_ge(gelu_done, (b * FT + f) * 2 + 1)
                        for part in (0, 1):
                            pe.matmul(down_ps[t][:, :], w2_split[part][:, f, cols], act_hi[i][:, f, :],
                                      start=(f + part == 0), stop=False)
                    for f in range(FT):
                        if t == 0:
                            pe.wait_ge(act_split, b * FT + f + 1)
                        m = pe.matmul(down_ps[t][:, :], w2_split[0][:, f, cols], act_lo[i][:, f, :],
                                      start=False, stop=(f == FT - 1))
                    m.then_inc(down_made, 1)

                def turn(b, i):
                    up(b, 0)
                    if not is_last(b):
                        transpose_in_f(b + 1, 1 - i, 0)
                        transpose_in_f(b + 1, 1 - i, 1)
                    up(b, 1)
                    if isinstance(b, int) and b == 1:
                        out_proj(B - 1, 0, end=True)
                    if not zero(b):
                        down(b - 1, 1 - i, 0)
                    up(b, 2)
                    if isinstance(b, int) and b == 1:
                        out_proj(B - 1, 1, end=True)
                    up(b, 3)
                    if not is_last(b):
                        transpose_out_f(b + 1, 0)
                        transpose_out_f(b + 1, 1)
                    if not zero(b):
                        down(b - 1, 1 - i, 1)

                def out_proj(b, t, end=False):
                    if t == 0:
                        pe.wait_ge(ctx_rounded, b * CT + CT)
                    if t == 0:
                        pe.wait_ge(mlo_done, b * NG + NG + (0 if end else 3))
                    else:
                        pe.wait_ge(r_done, b * CT + 1)
                    cols = slice(t * P, (t + 1) * P)
                    for k in range(CT):
                        for part in (0, 1):
                            pe.matmul(xc_ps[:, :], w_split["o"][:, part, k, cols], ctx_parts[:, 0, k, :],
                                      start=(k + part == 0), stop=False)
                    if t == 0:
                        pe.wait_ge(ctx_rest_done, b * CT + CT)
                    for k in range(CT):
                        m = pe.matmul(xc_ps[:, :], w_split["o"][:, 0, k, cols], ctx_parts[:, 1, k, :],
                                      start=False, stop=(k == CT - 1))
                    m.then_inc(wo_made, 1)

                def batch(b, first=False, last=False, more=True):
                    for s in range(STEPS):
                        q = s + LEAD
                        nb, nq = (b, q) if q < STEPS else (b + 1, q - STEPS)
                        todo = q < STEPS or not last
                        for j in (0, 1):
                            scores(b, s, j, first)
                            if todo:
                                max_scores(nb, nq, j)
                        if s:
                            prob_value(b, s - 1, first)
                        elif not first:
                            prob_value(b - 1, STEPS - 1)
                        if s % KC == 2:
                            if s + 2 < STEPS:
                                transpose_max(b, (s + 2) // KC, first)
                            elif not last:
                                transpose_max(b + 1, 0)
                        if s == 0 and not last:
                            for t in range(CT):
                                transpose_out(b + 1, "k", t)
                        for j in (2, 3):
                            scores(b, s, j, first)
                            if todo:
                                max_scores(nb, nq, j)
                        if s in (7, 8) and not first:
                            out_proj(b - 1, s - 7)
                        if not last:
                            if s == 2:
                                for t in range(CT):
                                    transpose_out(b + 1, "q", t)
                            if s in (3, 5):
                                project(b + 1, "k", s // 5)
                            if s in (4, 6):
                                project(b + 1, "q", s // 6)
                            if s == 13:
                                make_v(b + 1, 0)
                        if more and s in (9, 10, 11, 12):
                            transpose_in(b + 2, "k" if s < 11 else "q", (s - 9) % 2)
                        if s == 15 and not last:
                            make_v(b + 1, 1)
                        if s == 0 and not first:
                            make_v(b, 2)
                        if s == 1:
                            make_v(b, 3)
                        if last and s == 12:
                            transpose_in_f(0, 0, 0)
                            transpose_in_f(0, 0, 1)

                pe.wait_ge(consts, 5)
                for n in "kq":
                    for half in range(2):
                        transpose_in(0, n, half)
                for n in "kq":
                    for t in range(CT):
                        transpose_out(0, n, t)
                pe.wait_ge(weights, 11 * DMA)
                pe.wait_ge(w_lo_done, 4)
                for t in range(CT):
                    for n in "kq":
                        project(0, n, t)
                for c in range(3):
                    make_v(0, c)
                    if c < 2:
                        transpose_in(1, "k", c)
                for half in range(2):
                    transpose_in(1, "q", half)
                pe.wait_ge(consts, 6)
                pe.wait_ge(cleared, 2)
                for q in range(LEAD):
                    for j in range(HG):
                        max_scores(0, q, j, fresh=True)
                        if (q, j) == (KC, 2):
                            transpose_max(0, 0, first=True)
                    if q == KC - 1:
                        pe.wait_ge(cleared, 4)
                batch(0, first=True)
                with pe.Fori(1, B - 2) as b:
                    batch(b)
                batch(B - 2, more=False)
                batch(B - 1, last=True, more=False)
                prob_value(B - 1, STEPS - 1)
                transpose_out_f(0, 0)
                transpose_out_f(0, 1)
                pe.wait_ge(mx_done, B * UNITS)
                pe.wait_ge(ffw_split, 4)
                turns(pe, turn)
                down(B - 1, 1, 0)
                down(B - 1, 1, 1)


_INS = ['x', 'ctx_2048', 'L0_xattn_Wq', 'L0_xattn_Wk', 'L0_xattn_Wv', 'L0_xattn_Wo', 'L0_xattn_ln_q_g',
        'L0_xattn_ln_q_b', 'L0_xattn_ln_kv_g', 'L0_xattn_ln_kv_b', 'L0_xattn_ffn_ln_g', 'L0_xattn_ffn_ln_b',
        'L0_xattn_W1', 'L0_xattn_b1', 'L0_xattn_W2', 'L0_xattn_b2']
_OUTS = [((16, 256, 512), 'float32')]


def positions(c, t):
    import math
    import numpy as np
    f = np.float32
    div = np.exp((np.arange(0, c, 2, dtype=f) * f(-math.log(10000.0) / c)).astype(np.float64)).astype(f)
    ang = (np.arange(t, dtype=f)[:, None] * div).astype(np.float64)
    pe = np.zeros((t, c), f)
    pe[:, 0::2] = np.sin(ang)
    pe[:, 1::2] = np.cos(ang)
    return np.ascontiguousarray(pe.T)


def kernel(**inputs):
    import numpy as _np
    import concourse.bacc as _bacc
    from concourse import mybir as _mybir
    from concourse.bass_utils import run_bass_kernel_spmd as _run

    nc = _bacc.Bacc("TRN2", target_bir_lowering=False, num_devices=1)
    arrays, args = {}, []
    for name in _INS:
        a = _np.ascontiguousarray(inputs[name])
        arrays[f"in_{name}_dram"] = a
        args.append(nc.dram_tensor(f"in_{name}_dram", a.shape, _mybir.dt.from_np(a.dtype), kind="ExternalInput").ap())
    table = positions(inputs["x"].shape[1], inputs["x"].shape[2])
    arrays["in_positions_dram"] = table
    args.append(nc.dram_tensor("in_positions_dram", table.shape, _mybir.dt.from_np(table.dtype), kind="ExternalInput").ap())
    for i, (shape, dtype) in enumerate(_OUTS):
        dt = _mybir.dt.from_np(_np.dtype(dtype))
        args.append(nc.dram_tensor(f"out_{i}_dram", shape, dt, kind="ExternalOutput").ap())
    xattn_kernel(nc, *args)
    r = _run(nc, [arrays], core_ids=[0])
    return r.results[0]["out_0_dram"]
```
